# Optimizing a Trainium2 kernel written in Bass

```python
import numpy as np
import jax
import jax.numpy as jnp

def _softmax(x, axis=-1):
    return jax.nn.softmax(x, axis=axis)

def _gelu(x):
    return jax.nn.gelu(x, approximate=True)

def _silu(x):
    return jax.nn.silu(x)

def _sigmoid(x):
    return jax.nn.sigmoid(x)

def _layernorm(x, axis=-1, eps=1e-05):
    m = jnp.mean(x, axis=axis, keepdims=True)
    v = jnp.var(x, axis=axis, keepdims=True)
    return (x - m) / jnp.sqrt(v + eps)

def _scatter_add(tgt, idx, src, axis=0):
    return tgt.at[idx].add(src)

def _segment_sum(src, seg, n):
    return jax.ops.segment_sum(src, seg, n)
kernel_name = 'mk_flamingo_gated_d1_seqx_r8_9386bf'

def setup_inputs(seed: int=0):
    np.random.seed(seed)
    _w = jnp.asarray

    def _rec_inputs():
        import jax
        import jax.numpy as jnp
        _rk = jax.random.key(seed)
        x = 7.22e-05 + 1 * jax.random.normal(jax.random.fold_in(_rk, 1), (64, 64, 256), jnp.float32)
        _lenS = 64 - jax.random.randint(jax.random.fold_in(_rk, 7), (64,), 0, max(1, 64 // 4) + 1, jnp.int32)
        _lenS2 = 64 - jax.random.randint(jax.random.fold_in(_rk, 8), (64,), 0, max(1, 64 // 4) + 1, jnp.int32)
        _ctx_1024P = jax.random.normal(jax.random.fold_in(_rk, 11), (64, 16, 128), jnp.float32)
        _ctx_1024c = jax.random.dirichlet(jax.random.fold_in(_rk, 511), 0.3 * jnp.ones((16,), jnp.float32), (64, 64))
        _ctx_1024t = jnp.einsum('bsk,bkd->bsd', _ctx_1024c, _ctx_1024P)
        _ctx_1024t = _ctx_1024t * jax.lax.rsqrt(jnp.mean(jnp.square(_ctx_1024t)) + 1e-12) * 0.953939
        ctx_1024 = -0.000673644 + 1.00013 * (_ctx_1024t + 0.3 * jax.random.normal(jax.random.fold_in(_rk, 611), (64, 64, 128), jnp.float32))
        _g = jax.random.normal(jax.random.fold_in(_rk, 9001), (2, 1), jnp.float32)
        _g = jnp.sign(_g) * jnp.maximum(jnp.abs(_g), 1.0) + (_g == 0) * 1.0
        g_xattn = _g[0]
        g_ffn = _g[1]
        return (x, ctx_1024, g_xattn, g_ffn)
    x, ctx_1024, g_xattn, g_ffn = _rec_inputs()

    def _L0_xattn_setup():
        import jax, jax.numpy as jnp
        import numpy as np
        B, S1, S2, DCA = (2, 256, 128, 16)
        QDIM, KDIM, H = (256, 128, 16)
        HD = QDIM // H
        SCALE = HD ** (-0.5)
        EPS = 1e-06
        DCA_WEIGHT = 1.0

        def _ln(t, w, b):
            m = jnp.mean(t, axis=-1, keepdims=True)
            v = jnp.var(t, axis=-1, keepdims=True)
            return (t - m) * jax.lax.rsqrt(v + EPS) * w + b

        def _attn(q, k, v):
            s = jnp.einsum('bhqd,bhkd->bhqk', q, k) * SCALE
            p = jax.nn.softmax(s, axis=-1)
            return jnp.einsum('bhqk,bhkd->bhqd', p, v)
        key = jax.random.key(seed)
        ks = jax.random.split(key, 8)
        w = lambda k, shape: jax.random.normal(k, shape, jnp.float32) * 0.02
        return {'x': jax.random.normal(ks[0], (B, S1, QDIM), jnp.float32), 'y': jax.random.normal(ks[1], (B, S2 + DCA, KDIM), jnp.float32), 'Wq': w(ks[2], (QDIM, QDIM)), 'bq': jnp.zeros((QDIM,), jnp.float32), 'Wk': w(ks[3], (KDIM, QDIM)), 'bk': jnp.zeros((QDIM,), jnp.float32), 'Wv': w(ks[4], (KDIM, QDIM)), 'bv': jnp.zeros((QDIM,), jnp.float32), 'Wkv_dca': w(ks[5], (KDIM, 2 * QDIM)), 'bkv_dca': jnp.zeros((2 * QDIM,), jnp.float32), 'qn_w': jnp.ones((HD,), jnp.float32), 'qn_b': jnp.zeros((HD,), jnp.float32), 'kn_w': jnp.ones((HD,), jnp.float32), 'kn_b': jnp.zeros((HD,), jnp.float32), 'kn_dca_w': jnp.ones((HD,), jnp.float32), 'kn_dca_b': jnp.zeros((HD,), jnp.float32), 'Wo': w(ks[6], (QDIM, QDIM)), 'bo': jnp.zeros((QDIM,), jnp.float32)}
    _L0_xattn_all = _L0_xattn_setup()
    _L0_xattn_in = {k: v for k, v in _L0_xattn_all.items() if k in ('Wq', 'bq', 'Wk', 'bk', 'Wv', 'bv', 'Wkv_dca', 'bkv_dca', 'qn_w', 'qn_b', 'kn_w', 'kn_b', 'kn_dca_w', 'kn_dca_b', 'Wo', 'bo')}
    del _L0_xattn_all

    def _L0_ffn_setup():
        import jax, jax.numpy as jnp
        import numpy as np
        B, S, H = (2, 128, 256)
        E, K, F = (8, 2, 176)
        N_SHARED = 2
        FS = F * N_SHARED
        ROUTED_SCALE = 1.0

        def _swiglu_mlp(x, wg, wu, wd):
            return jax.nn.silu(x @ wg.T) * (x @ wu.T) @ wd.T
        key = jax.random.key(seed)
        ks = jax.random.split(key, 8)

        def w(k, shape, fan_in):
            return jax.random.normal(k, shape, jnp.float32) * (1.0 / np.sqrt(fan_in))
        return {'hidden_states': jax.random.normal(ks[0], (B, S, H), jnp.float32), 'gate_weight': w(ks[1], (E, H), H), 'w_gate': w(ks[2], (E, F, H), H), 'w_up': w(ks[3], (E, F, H), H), 'w_down': w(ks[4], (E, H, F), F), 'sw_gate': w(ks[5], (FS, H), H), 'sw_up': w(ks[6], (FS, H), H), 'sw_down': w(ks[7], (H, FS), FS)}
    _L0_ffn_all = _L0_ffn_setup()
    _L0_ffn_in = {k: v for k, v in _L0_ffn_all.items() if k in ('gate_weight', 'w_gate', 'w_up', 'w_down', 'sw_gate', 'sw_up', 'sw_down')}
    del _L0_ffn_all
    return {'x': x, 'ctx_1024': ctx_1024, 'g_xattn': g_xattn, 'g_ffn': g_ffn, 'L0_xattn_Wq': _L0_xattn_in['Wq'], 'L0_xattn_bq': _L0_xattn_in['bq'], 'L0_xattn_Wk': _L0_xattn_in['Wk'], 'L0_xattn_bk': _L0_xattn_in['bk'], 'L0_xattn_Wv': _L0_xattn_in['Wv'], 'L0_xattn_bv': _L0_xattn_in['bv'], 'L0_xattn_Wkv_dca': _L0_xattn_in['Wkv_dca'], 'L0_xattn_bkv_dca': _L0_xattn_in['bkv_dca'], 'L0_xattn_qn_w': _L0_xattn_in['qn_w'], 'L0_xattn_qn_b': _L0_xattn_in['qn_b'], 'L0_xattn_kn_w': _L0_xattn_in['kn_w'], 'L0_xattn_kn_b': _L0_xattn_in['kn_b'], 'L0_xattn_kn_dca_w': _L0_xattn_in['kn_dca_w'], 'L0_xattn_kn_dca_b': _L0_xattn_in['kn_dca_b'], 'L0_xattn_Wo': _L0_xattn_in['Wo'], 'L0_xattn_bo': _L0_xattn_in['bo'], 'L0_ffn_gate_weight': _L0_ffn_in['gate_weight'], 'L0_ffn_w_gate': _L0_ffn_in['w_gate'], 'L0_ffn_w_up': _L0_ffn_in['w_up'], 'L0_ffn_w_down': _L0_ffn_in['w_down'], 'L0_ffn_sw_gate': _L0_ffn_in['sw_gate'], 'L0_ffn_sw_up': _L0_ffn_in['sw_up'], 'L0_ffn_sw_down': _L0_ffn_in['sw_down']}

def reference(x, ctx_1024, g_xattn, g_ffn, L0_xattn_Wq, L0_xattn_bq, L0_xattn_Wk, L0_xattn_bk, L0_xattn_Wv, L0_xattn_bv, L0_xattn_Wkv_dca, L0_xattn_bkv_dca, L0_xattn_qn_w, L0_xattn_qn_b, L0_xattn_kn_w, L0_xattn_kn_b, L0_xattn_kn_dca_w, L0_xattn_kn_dca_b, L0_xattn_Wo, L0_xattn_bo, L0_ffn_gate_weight, L0_ffn_w_gate, L0_ffn_w_up, L0_ffn_w_down, L0_ffn_sw_gate, L0_ffn_sw_up, L0_ffn_sw_down):
    import jax
    import jax.numpy as jnp

    def _L0_xattn_ref(x, y, Wq, bq, Wk, bk, Wv, bv, Wkv_dca, bkv_dca, qn_w, qn_b, kn_w, kn_b, kn_dca_w, kn_dca_b, Wo, bo):
        import jax, jax.numpy as jnp
        import numpy as np
        B, S1, S2, DCA = (2, 256, 128, 16)
        QDIM, KDIM, H = (256, 128, 16)
        HD = QDIM // H
        SCALE = HD ** (-0.5)
        EPS = 1e-06
        DCA_WEIGHT = 1.0

        def _ln(t, w, b):
            m = jnp.mean(t, axis=-1, keepdims=True)
            v = jnp.var(t, axis=-1, keepdims=True)
            return (t - m) * jax.lax.rsqrt(v + EPS) * w + b

        def _attn(q, k, v):
            s = jnp.einsum('bhqd,bhkd->bhqk', q, k) * SCALE
            p = jax.nn.softmax(s, axis=-1)
            return jnp.einsum('bhqk,bhkd->bhqd', p, v)
        b, s1, _ = x.shape
        y_dca = y[:, -DCA:, :]
        y_main = y[:, :-DCA, :]
        kv_dca = (y_dca @ Wkv_dca + bkv_dca).reshape(b, DCA, 2, H, HD)
        k_dca = _ln(kv_dca[:, :, 0], kn_dca_w, kn_dca_b)
        v_dca = kv_dca[:, :, 1]
        s2 = y_main.shape[1]
        q = _ln((x @ Wq + bq).reshape(b, s1, H, HD), qn_w, qn_b)
        kv = jnp.concatenate([y_main @ Wk + bk, y_main @ Wv + bv], axis=-1)
        kv = kv.reshape(b, s2, H, 2 * HD)
        k = _ln(kv[..., :HD], kn_w, kn_b)
        v = kv[..., HD:]
        qT = q.transpose(0, 2, 1, 3)
        ctx = _attn(qT, k.transpose(0, 2, 1, 3), v.transpose(0, 2, 1, 3))
        ctx = ctx.transpose(0, 2, 1, 3).reshape(b, s1, QDIM)
        ctx_dca = _attn(qT, k_dca.transpose(0, 2, 1, 3), v_dca.transpose(0, 2, 1, 3))
        ctx_dca = ctx_dca.transpose(0, 2, 1, 3).reshape(b, s1, QDIM)
        ctx = ctx + DCA_WEIGHT * ctx_dca
        return ctx @ Wo + bo

    def _L0_ffn_ref(hidden_states, gate_weight, w_gate, w_up, w_down, sw_gate, sw_up, sw_down):
        import jax, jax.numpy as jnp
        import numpy as np
        B, S, H = (2, 128, 256)
        E, K, F = (8, 2, 176)
        N_SHARED = 2
        FS = F * N_SHARED
        ROUTED_SCALE = 1.0

        def _swiglu_mlp(x, wg, wu, wd):
            return jax.nn.silu(x @ wg.T) * (x @ wu.T) @ wd.T
        b, s, h = hidden_states.shape
        x = hidden_states.reshape(-1, h)
        T = x.shape[0]
        logits = x.astype(jnp.float32) @ gate_weight.astype(jnp.float32).T
        scores = jax.nn.softmax(logits, axis=-1)
        topk_w, topk_idx = jax.lax.top_k(scores, K)
        topk_w = topk_w / (jnp.sum(topk_w, axis=-1, keepdims=True) + 1e-20)
        topk_w = topk_w * ROUTED_SCALE
        cw = jnp.zeros((T, E), jnp.float32).at[jnp.arange(T)[:, None], topk_idx].add(topk_w)
        g = jax.nn.silu(jnp.einsum('th,efh->tef', x, w_gate)) * jnp.einsum('th,efh->tef', x, w_up)
        expert_out = jnp.einsum('tef,ehf->teh', g, w_down)
        y = jnp.einsum('te,teh->th', cw, expert_out).reshape(b, s, h)
        y = y + _swiglu_mlp(x, sw_gate, sw_up, sw_down).reshape(b, s, h)
        return y
    x = x + jnp.tanh(g_xattn[0]) * _L0_xattn_ref(_layernorm(x, axis=-1), ctx_1024, L0_xattn_Wq, L0_xattn_bq, L0_xattn_Wk, L0_xattn_bk, L0_xattn_Wv, L0_xattn_bv, L0_xattn_Wkv_dca, L0_xattn_bkv_dca, L0_xattn_qn_w, L0_xattn_qn_b, L0_xattn_kn_w, L0_xattn_kn_b, L0_xattn_kn_dca_w, L0_xattn_kn_dca_b, L0_xattn_Wo, L0_xattn_bo)
    x = x + jnp.tanh(g_ffn[0]) * _L0_ffn_ref(_layernorm(x, axis=-1), L0_ffn_gate_weight, L0_ffn_w_gate, L0_ffn_w_up, L0_ffn_w_down, L0_ffn_sw_gate, L0_ffn_sw_up, L0_ffn_sw_down)
    return x

_drawn_inputs = setup_inputs


def setup_inputs(seed=0):
    import zlib

    import numpy as np

    out = dict(_drawn_inputs(seed))
    spreads = {'L0_xattn_bq': (0.0, 0.376),
     'L0_xattn_bk': (0.0, 0.1),
     'L0_xattn_bv': (0.0, 0.1),
     'L0_xattn_bkv_dca': (0.0, 0.1),
     'L0_xattn_qn_w': (1.0, 0.6),
     'L0_xattn_qn_b': (0.0, 0.571),
     'L0_xattn_kn_w': (1.0, 0.6),
     'L0_xattn_kn_b': (0.0, 0.8),
     'L0_xattn_kn_dca_w': (1.0, 0.6),
     'L0_xattn_kn_dca_b': (0.0, 0.8),
     'L0_xattn_bo': (0.0, 0.1)}
    factors = {}
    for name, (base, spread) in spreads.items():
        noise = np.random.default_rng([zlib.crc32(name.encode()), seed]).standard_normal(out[name].shape)
        drawn = base * np.exp(spread * noise) if base else spread * noise
        out[name] = jnp.asarray(drawn.astype(out[name].dtype))
    for name, factor in factors.items():
        out[name] = (out[name] * factor).astype(out[name].dtype)
    return out
```

```python
from contextlib import ExitStack

import concourse.bass as bass
from concourse import mybir

ALU = mybir.AluOpType
ACT = mybir.ActivationFunctionType
AX = mybir.AxisListType
F32 = mybir.dt.float32
F32R = mybir.dt.float32r
I32 = mybir.dt.int32
P = 128


def gated_cross_attention_and_moe(nc, a, out):
    T, D = a["x"].shape
    NS = 64
    NQ = T // NS
    NM, ND = 48, 16
    NK = NM + ND
    HD = 16
    H = D // HD
    NT = T // P
    DC = D // P
    G = P // 32
    SCALE = float(HD) ** -0.5
    RSQRT_SEED = 0x5F3759DF
    E, _, _, _ = a["w_gu"].shape
    F = a["w_gu"].shape[3] // 2
    FS = a["s_gu"].shape[2] // 2
    NE = (2 * T + E * (P - 1)) // P
    NE += NE % 2
    CUTS = {"sh": [(k, min(k + P, FS)) for k in range(0, FS, P)], "ex": [(k, min(k + P, F)) for k in range(0, F, P)]}

    with ExitStack() as ctx:
        def sb(name, shape, dt=F32):
            return ctx.enter_context(nc.sbuf_tensor(name, shape, dt))

        def pb(name, shape, dt=F32):
            return ctx.enter_context(nc.psum_tensor(name, shape, dt))

        def sem(name):
            return ctx.enter_context(nc.semaphore(name))

        ident = sb("ident", [P, P])
        wq = sb("wq", [P, DC, D])
        wkm = sb("wkm", [P, D])
        wvm = sb("wvm", [P, D])
        wkd = sb("wkd", [P, D])
        wvd = sb("wvd", [P, D])
        wo = sb("wo", [P, DC, D])
        rows = sb("rows", [4, 4 * D])
        ones_h = sb("ones_h", [P, P])
        vecs = sb("vecs", [P, 6])
        gates = sb("gates", [P, 2])
        tg = sb("tg", [P, 2])
        par_mask = sb("par_mask", [P, 2])
        kvec = sb("kvec", [P, 2, 4])
        csum = sb("csum", [P, 4, H])
        bsum = sb("bsum", [4, 2 * H])
        gateT = sb("gateT", [P, DC, E])
        tri = sb("tri", [P, P])
        ones = sb("ones", [P, P])
        e_idx = sb("e_idx", [P, E])
        j_idx = sb("j_idx", [P, NE])
        gu = [sb(f"gu_{n}", [P, DC, E * 2 * F], F32R) for n in "hl"]
        dn = [sb(f"dn_{n}", [P, 2, E * D], F32R) for n in "hl"]
        sgu = [sb(f"sgu_{n}", [P, DC, 2 * FS], F32R) for n in "hl"]
        sdn = [sb(f"sdn_{n}", [P, 3, D], F32R) for n in "hl"]
        stage = sb("stage", [P, 2, DC * 2 * F])
        xTs = [sb(f"xT_{n}", [P, 2, DC, P], F32R) for n in "hl"]
        hTs = [sb(f"hT_{n}", [P, 2, 3, P], F32R) for n in "hl"]
        idx = sb("idx", [P, 2, 2], mybir.dt.uint32)
        c15 = sb("c15", [P, 2 * H])
        zero_row = sb("zero_row", [P, D])
        X = sb("X", [P, NT, D])
        st1 = sb("st1", [P, NT, 6])
        mv1 = sb("mv1", [P, NT, 2])
        rstd1 = sb("rstd1", [P, NT])
        rstd2 = sb("rstd2", [P, NT])
        st2 = sb("st2", [P, 2, 6])
        mvr = sb("mvr", [P, 2, 2])
        mv2 = sb("mv2", [P, NT, 2])
        ARENA = 12 * 1024
        arena = sb("arena", [P, ARENA])
        used = [0]

        def take(*shape, dt=F32):
            n = 1
            for d in shape:
                n *= d
            at, used[0] = used[0], used[0] + n
            assert used[0] <= ARENA
            ap = arena[:, at:at + n]
            if dt != F32:
                ap = ap.bitcast(dt)
            names = "abcde"[:len(shape)]
            return ap.rearrange("p (" + " ".join(names) + ") -> p " + " ".join(names),
                                **dict(zip(names, shape))) if len(shape) > 1 else ap

        y_in = take(2, P)
        yM = take(2, 2, NK)
        yD = take(2, 2, NK)
        xn = take(2, D)
        xnT = take(2, DC, P)
        sq = take(2, 2 * D)
        var = take(2, 2 * H)
        hv = take(2, 2 * H)
        seed = take(2, 2 * H, dt=I32)
        ya = take(2, 2 * H)
        yt = take(2, 2 * H)
        qk = take(2, 2 * D)
        qT = take(2, DC, P)
        kT = take(2, DC * 2, 2, NK).rearrange("p b (c h) s k -> p b c h s k", c=DC)
        vbd = take(2, 2, H // 2, 2 * HD).rearrange("p b s j (h d) -> p b s j h d", h=2)
        S = take(2, G, 4, NK)
        mx = take(2, 2, G, 4)
        den = take(2, 2, H)
        PT = take(2, G, DC, P)
        cT = take(2, DC, P)
        xm = take(2, D)
        used[0] = 0
        x2 = take(2, D)
        x2T = take(2, DC, P)
        sg = take(2, FS)
        hid = take(2, FS)
        rows_in = take(4, D)
        y_sb = take(2, D)
        g1 = take(2, D)
        g2 = take(2, D)
        lg = take(NT, E)
        oh1 = take(NT, E)
        oh2 = take(NT, E)
        both = take(NT, E)
        pfx = take(NT, E)
        cumA = take(NT, E)
        cumB = take(NT, E)
        cand = take(NT, E)
        r1 = take(NT)
        r2 = take(NT)
        w1 = take(NT)
        w2 = take(NT)
        wsum = take(NT)
        pos1f = take(NT)
        pos2f = take(NT)
        pos1 = take(NT, dt=I32)
        pos2 = take(NT, dt=I32)
        tiles_f = take(E)
        tiles_i = take(E, dt=I32)
        endA = take(E)
        endB = take(E)
        start = take(E)
        ge_end = take(NE, E)
        te_f = take(NE)
        te = take(NE, dt=I32)

        pS = pb("pS", [P, G, 512])
        p_sc = pS[:, :, 0:256]
        p_pt = pS[:, :, 256:512]
        pQK = pb("pQK", [P, 512])
        pV = pb("pV", [P, 512])
        p_v = pV[:, 0:D]
        pT = pb("pT", [P, 2, DC, P])
        p_x = pT[:, 0].rearrange("p c n -> p (c n)")
        pCO = pb("pCO", [P, 512])
        p_c = pCO[:, 0:256].rearrange("p (c n) -> p c n", c=DC)
        p_o = pCO[:, 256:512]

        s_w = sem("weights_loaded")
        s_x = [sem(f"x_loaded{n}") for n in range(4)]
        s_id = sem("identity_made")
        s_ws = [sem(f"staged{n}") for n in range(2)]
        s_split, s_ready = sem("weights_split"), sem("ffn_weights_ready")
        s_zf = sem("rows_zeroed")
        s_v2, s_rt2, s_r2 = sem("ln2_var"), sem("ln2_roots"), sem("ln2_rstd")
        s_n2, s_t2, s_e2, s_lg = sem("x2_ready"), sem("x2T_in_psum"), sem("x2T_ready"), sem("logits_ready")
        s_rx, s_rs_, s_oh, s_cnt = sem("router_exp_in"), sem("router_step"), sem("choices_ready"), sem("counts_ready")
        s_re, s_pos = sem("router_exp"), sem("positions_ready")
        s_sc1 = [sem(f"rows_scattered{n}") for n in range(2)]
        s_xs = [sem(f"expert_rows_loaded{n}") for n in range(4)]
        s_ys = [sem(f"expert_rows_stored{n}") for n in range(2)]
        s_g = [sem(f"rows_gathered{n}") for n in range(2)]
        s_idx = sem("places_copied")
        s_cmb, s_o1 = sem("combined"), sem("first_added")
        s_os = [sem(f"tile_stored{n}") for n in range(2)]
        ffn = {k: {n: sem(f"{k}_{n}") for n in
                   ("x", "xt", "xh", "xl", "gu", "silu", "h", "ht", "hh", "hl", "y", "yd")} for k in ("sh", "ex")}
        s_yl = [sem(f"y_loaded{n}") for n in range(2)]
        s_y = sem("y_spread")
        s_cen = sem("weights_centred")
        s_c = sem("centring_step")
        s_zero = sem("zeros_written")
        s_st = sem("ln1_stats")
        s_rt = sem("ln1_roots")
        s_r1 = sem("ln1_rstd")
        s_tg = sem("gates_ready")
        s_xn, s_tx, s_xe = sem("xn_ready"), sem("xnT_in_psum"), sem("xnT_ready")
        s_proj, s_sq, s_vev = sem("projected"), sem("squared"), sem("v_ready")
        s_vr, s_seed, s_var = sem("var_summed"), sem("seed_shifted"), sem("seed_ready")
        s_nw, s_rs = sem("newton_step"), sem("rstd_ready")
        s_qk, s_tq, s_qe = sem("qk_normed"), sem("qkT_in_psum"), sem("qkT_ready")
        s_sc, s_max, s_mx = sem("scores_ready"), sem("max_ready"), sem("max_subtracted")
        s_ex, s_sum, s_rd = sem("exp_ready"), sem("sums_ready"), sem("reciprocal_ready")
        s_nm, s_pt, s_pe = sem("probs_ready"), sem("probsT_in_psum"), sem("probsT_ready")
        s_pv, s_ce, s_wo = sem("ctxT_in_psum"), sem("ctxT_ready"), sem("attn_out")
        s_res, s_b2, s_l2 = sem("residual_added"), sem("ln2_bn"), sem("ln2_stats")
        s_out = sem("out_written")

        s_passed = {nc.gpsimd: sem("pool_passed"), nc.tensor: sem("pe_passed")}

        block = ctx.enter_context(nc.Block())

        def ge(eng, s, value):
            if not isinstance(value, int) or value > 0:
                eng.wait_ge(s, value)

        def settle(eng):
            eng.sem_inc(s_passed[eng], 1)

        def over_tiles(eng, step, n=NT, unroll=2):
            first = 4
            rounds = (n - 2 - first) // unroll
            for i in range(first):
                step(i, i % unroll)
            with eng.Fori(first // unroll, first // unroll + rounds) as r:
                for b in range(unroll):
                    step(r * unroll + b, b)
            for i in range(first + rounds * unroll, n + 2):
                step(i, i % unroll)

        def real(t, n=NT):
            return not isinstance(t, int) or 0 <= t < n

        def heads(ap):
            return ap.rearrange("p (h d) -> p h d", d=HD)

        xs = nc.dram_tensor("rows_by_expert", [NE * P, D], F32, kind="Internal").ap()
        ys = nc.dram_tensor("outputs_by_expert", [NE * P, D], F32, kind="Internal").ap()

        def row_tile(dram, t):
            return dram[t * P:(t + 1) * P, :] if isinstance(t, int) else dram[bass.ts(t, P), :]

        bank = [pS[:, 0, :], pS[:, 1, :], pS[:, 2, :], pS[:, 3, :], pQK[:], pV[:],
                pT[:].rearrange("p a c n -> p (a c n)"), pCO[:]]

        def gate_up(k, b):
            if k == "sh":
                return bank[2 * b][:, 0:FS], bank[2 * b + 1][:, 0:FS]
            return bank[2 * b][:, 0:F], bank[2 * b][:, F:2 * F]

        p_xT, p_hT, p_y = bank[4], bank[5], bank[6]

        def ffn_pe(pe, k, n):
            s, cuts = ffn[k], CUTS[k]

            def products(dst, pairs):
                last = len(pairs) - 1
                for m, ((xh, xl), (wh, wl)) in enumerate(pairs):
                    pe.matmul(dst, xh, wl, start=(m == 0), stop=False)
                    pe.matmul(dst, xl, wh, start=False, stop=False)
                    r = pe.matmul(dst, xh, wh, start=False, stop=(m == last))
                return r

            def step(i, b):
                b2, o = b % 2, 1 - b % 2
                def transpose_x(t, tb):
                    if k == "sh":
                        pe.wait_ge(s["x"], t + 1)
                        src = x2[:, tb % 2, :]
                    else:
                        pe.wait_ge(s_xs[tb], (t - tb) * 4 + 16 if not isinstance(t, int) else (t // 4 + 1) * 16)
                        src = rows_in[:, tb, :]
                    ge(pe, s["xl"], t)
                    for c in range(DC):
                        m = pe.transpose(p_xT[:, c * P:(c + 1) * P], src[:, c * P:(c + 1) * P], ident[:])
                    m.then_inc(s["xt"], 1)

                if isinstance(i, int) and i == 0:
                    transpose_x(0, 0)
                if real(i + 1, n):
                    transpose_x(i + 1, o if k == "sh" else (b + 1) % 4)
                if real(i - 1, n):
                    pe.wait_ge(s["h"], i)
                    ge(pe, s["hl"], i - 1)
                    for m, (k0, k1) in enumerate(cuts):
                        r = pe.transpose(p_hT[0:k1 - k0, m * P:(m + 1) * P], hid[:, o, k0:k1], ident[:])
                    r.then_inc(s["ht"], 1)
                if real(i, n):
                    pe.wait_ge(s["xl"], i + 1)
                    ge(pe, s["h"], i - 1)
                    x = [(xTs[0][:, b2, c, :], xTs[1][:, b2, c, :]) for c in range(DC)]
                    if k == "sh":
                        for m, dst in enumerate(gate_up(k, b2)):
                            r = products(dst, [(x[c], [w[:, c, m * FS:(m + 1) * FS] for w in sgu]) for c in range(DC)])
                    else:
                        settle(pe)
                        e = pe.value_load(te[0:1, i:i + 1] if isinstance(i, int) else te[0:1, bass.ds(i, 1)],
                                          min_val=0, max_val=E - 1)
                        cols = bass.ds(e * (2 * F), 2 * F)
                        r = products(bank[2 * b2][:, 0:2 * F], [(x[c], [w[:, c, cols] for w in gu]) for c in range(DC)])
                    r.then_inc(s["gu"], 1)
                if real(i - 1, n):
                    pe.wait_ge(s["hl"], i)
                    ge(pe, s["yd"], i - 1)
                    h = [(hTs[0][0:k1 - k0, o, m, :], hTs[1][0:k1 - k0, o, m, :]) for m, (k0, k1) in enumerate(cuts)]
                    if k == "sh":
                        w = [[w[0:k1 - k0, m, :] for w in sdn] for m, (k0, k1) in enumerate(cuts)]
                    else:
                        settle(pe)
                        e = pe.value_load(te[0:1, i - 1:i] if isinstance(i, int) else te[0:1, bass.ds(i - 1, 1)],
                                          min_val=0, max_val=E - 1)
                        w = [[w[0:k1 - k0, m, bass.ds(e * D, D)] for w in dn] for m, (k0, k1) in enumerate(cuts)]
                    products(p_y[:, 0:D], list(zip(h, w))).then_inc(s["y"], 1)

            over_tiles(pe, step, n, 2 if k == "sh" else 4)

        def ffn_act(act, k, n):
            s, cuts = ffn[k], CUTS[k]

            def high_x(t, b):
                act.wait_ge(s["xt"], t + 1)
                ge(act, s["gu"], t - 1)
                act.activation(xTs[0][:, b].rearrange("p c n -> p (c n)"), p_xT[:, 0:D], ACT.Copy).then_inc(s["xh"], 1)

            def step(i, b):
                o = 1 - b
                if isinstance(i, int) and i == 0:
                    high_x(0, 0)
                if real(i + 1, n):
                    high_x(i + 1, o)
                if real(i - 1, n):
                    act.wait_ge(s["ht"], i)
                    ge(act, s["y"], i - 2)
                    for m, (k0, k1) in enumerate(cuts):
                        r = act.activation(hTs[0][0:k1 - k0, o, m, :], p_hT[0:k1 - k0, m * P:(m + 1) * P], ACT.Copy)
                    r.then_inc(s["hh"], 1)
                if real(i, n):
                    act.wait_ge(s["gu"], i + 1)
                    ge(act, s["h"], i - 1)
                    act.activation(sg[:, b, 0:cuts[-1][1]], gate_up(k, b)[0], ACT.Silu).then_inc(s["silu"], 1)
                if k == "ex" and real(i - 1, n):
                    act.wait_ge(s["y"], i)
                    ge(act, s_ys[o], (i - 1 - o) * 8 if not isinstance(i, int) else (i - 1) // 2 * 16)
                    act.activation(y_sb[:, o, :], p_y[:, 0:D], ACT.Copy).then_inc(s["yd"], 1)

            over_tiles(act, step, n)

        def ffn_dve(dve, k, n, make_x):
            s, cuts = ffn[k], CUTS[k]

            def rest_x(t, b):
                dve.wait_ge(s["xh"], t + 1)
                ge(dve, s["gu"], t - 1)
                dve.tensor_tensor(xTs[1][:, b].rearrange("p c n -> p (c n)"), p_xT[:, 0:D],
                                  xTs[0][:, b].rearrange("p c n -> p (c n)").bitcast(F32), ALU.subtract).then_inc(s["xl"], 1)

            def step(i, b):
                o = 1 - b
                if isinstance(i, int) and i == 0:
                    if make_x:
                        make_x(0, 0)
                        make_x(1, 1)
                    rest_x(0, 0)
                elif make_x and real(i + 1, n):
                    make_x(i + 1, o)
                if real(i + 1, n):
                    rest_x(i + 1, o)
                if real(i - 1, n):
                    dve.wait_ge(s["hh"], i)
                    ge(dve, s["y"], i - 2)
                    for m, (k0, k1) in enumerate(cuts):
                        r = dve.tensor_tensor(hTs[1][0:k1 - k0, o, m, :], p_hT[0:k1 - k0, m * P:(m + 1) * P],
                                              hTs[0][0:k1 - k0, o, m, :].bitcast(F32), ALU.subtract)
                    r.then_inc(s["hl"], 1)
                if real(i, n):
                    dve.wait_ge(s["silu"], i + 1)
                    ge(dve, s["ht"], i - 1)
                    w = cuts[-1][1]
                    dve.tensor_tensor(hid[:, b, 0:w], sg[:, b, 0:w], gate_up(k, b)[1], ALU.mult).then_inc(s["h"], 1)
                if k == "sh" and real(i - 1, n):
                    t = i - 1
                    dve.wait_ge(s["y"], i)
                    dve.scalar_tensor_tensor(out=X[:, t, :], in0=p_y[:, 0:D], scalar=tg[:, 1:2], in1=X[:, t, :],
                                             op0=ALU.mult, op1=ALU.add).then_inc(s["yd"], 1)

            over_tiles(dve, step, n)

        def route(dve):
            count = [0]

            def done(ins):
                count[0] += 1
                ins.then_inc(s_rs_, 1)
                dve.wait_ge(s_rs_, count[0])

            def over_e(v):
                return v.unsqueeze(2).broadcast_to([P, NT, E])

            def over_t(v):
                return v.unsqueeze(1).broadcast_to([P, NT, E])

            dve.wait_ge(s_lg, NT)
            p_lg = bank[7][:, 0:NT * E].rearrange("p (t e) -> p t e", e=E)
            done(dve.tensor_reduce(r1, p_lg, AX.X, ALU.max))
            dve.tensor_tensor(lg, p_lg, over_e(r1), ALU.subtract).then_inc(s_rx, 1)
            dve.wait_ge(s_re, 1)
            done(dve.tensor_reduce(r1, lg, AX.X, ALU.add))
            done(dve.reciprocal(r1, r1))
            done(dve.tensor_tensor(lg, lg, over_e(r1), ALU.mult))
            for w, oh in ((w1, oh1), (w2, oh2)):
                done(dve.tensor_reduce(w, lg, AX.X, ALU.max))
                done(dve.tensor_tensor(cand, lg, over_e(w), ALU.is_lt))
                done(dve.scalar_tensor_tensor(out=cand, in0=cand, scalar=float(E), in1=over_t(e_idx[:]), op0=ALU.mult, op1=ALU.add))
                done(dve.tensor_reduce(r2, cand, AX.X, ALU.min))
                done(dve.tensor_tensor(oh, over_t(e_idx[:]), over_e(r2), ALU.is_equal))
                if w is w1:
                    done(dve.scalar_tensor_tensor(out=lg, in0=oh, scalar=-2.0, in1=lg, op0=ALU.mult, op1=ALU.add))
            dve.tensor_tensor(both, oh1, oh2, ALU.add).then_inc(s_oh, 1)
            done(dve.tensor_tensor(wsum, w1, w2, ALU.add))
            done(dve.tensor_scalar(wsum, wsum, 1e-20, None, ALU.add))
            done(dve.reciprocal(wsum, wsum))
            done(dve.tensor_tensor(w1, w1, wsum, ALU.mult))
            done(dve.tensor_tensor(w2, w2, wsum, ALU.mult))
            dve.wait_ge(s_cnt, 1)
            done(dve.tensor_copy(pfx, bank[6][:, 0:NT * E].rearrange("p (t e) -> p t e", e=E)))
            done(dve.tensor_copy(cumA, bank[5][:, 0:NT * E].rearrange("p (t e) -> p t e", e=E)))
            done(dve.tensor_tensor(pfx, pfx, cumA, ALU.subtract))
            src, dst, d = cumA, cumB, 1
            while d < NT:
                done(dve.tensor_copy(dst[:, 0:d, :], src[:, 0:d, :]))
                done(dve.tensor_tensor(dst[:, d:NT, :], src[:, d:NT, :], src[:, 0:NT - d, :], ALU.add))
                src, dst, d = dst, src, 2 * d
            done(dve.tensor_tensor(pfx, pfx, src, ALU.add))
            done(dve.tensor_scalar(tiles_f, src[:, NT - 1, :], float(P - 1), None, ALU.add))
            done(dve.tensor_copy(tiles_i, tiles_f))
            done(dve.tensor_scalar(tiles_i, tiles_i, 7, None, ALU.arith_shift_right))
            done(dve.tensor_copy(tiles_f, tiles_i))
            done(dve.tensor_copy(endA, tiles_f))
            a_, b_, d = endA, endB, 1
            while d < E:
                done(dve.tensor_copy(b_[:, 0:d], a_[:, 0:d]))
                done(dve.tensor_tensor(b_[:, d:E], a_[:, d:E], a_[:, 0:E - d], ALU.add))
                a_, b_, d = b_, a_, 2 * d
            done(dve.tensor_tensor(start, a_, tiles_f, ALU.subtract))
            done(dve.tensor_scalar(start, start, float(P), None, ALU.mult))
            done(dve.tensor_tensor(pfx, pfx, over_t(start), ALU.add))
            for oh, pf, pos in ((oh1, pos1f, pos1), (oh2, pos2f, pos2)):
                done(dve.tensor_tensor(cand, oh, pfx, ALU.mult))
                done(dve.tensor_reduce(pf, cand, AX.X, ALU.add))
                done(dve.tensor_copy(pos, pf))
            done(dve.tensor_tensor(ge_end, j_idx[:].unsqueeze(2).broadcast_to([P, NE, E]),
                                   a_.unsqueeze(1).broadcast_to([P, NE, E]), ALU.is_ge))
            done(dve.tensor_reduce(te_f, ge_end, AX.X, ALU.add))
            done(dve.tensor_scalar(te_f, te_f, float(E - 1), None, ALU.min))
            dve.tensor_copy(te, te_f).then_inc(s_pos, 1)

        STAGED = []
        for e in range(E):
            STAGED.append((a["w_gu"][e], [w[:, :, 2 * F * e:2 * F * (e + 1)] for w in gu]))
            lo, hi = CUTS["ex"]
            STAGED.append((a["w_dn"][e, 0:P], [w[:, 0, D * e:D * (e + 1)] for w in dn]))
            STAGED.append((a["w_dn"][e, P:F], [w[0:F - P, 1, D * e:D * (e + 1)] for w in dn]))
        for c in range(DC):
            STAGED.append((a["s_gu"][c], [w[:, c, :] for w in sgu]))
        for n, (k0, k1) in enumerate(CUTS["sh"]):
            STAGED.append((a["s_dn"][k0:k1], [w[0:k1 - k0, n, :] for w in sdn]))

        def staged(n, shape):
            size = 1
            for d in shape[1:]:
                size *= d
            ap = stage[0:shape[0], n % 2, 0:size]
            return ap.rearrange("p (c n) -> p c n", c=shape[1]) if len(shape) > 2 else ap

        @block.sync
        def _(sp):
            for n in range(4):
                q = NT // 4
                sp.dma_start(X[:, n * q:(n + 1) * q, :],
                             a["x"].rearrange("(t p) d -> p t d", p=P)[:, n * q:(n + 1) * q, :]).then_inc(s_x[n], 16)
                if n == 0:
                    for dst, src in (
                        (wq, a["wq"].rearrange("(c p) n -> p c n", p=P)), (wkm, a["wkm"]), (wvm, a["wvm"]),
                        (wkd, a["wkd"]), (wvd, a["wvd"]), (wo, a["wo"].rearrange("(c p) n -> p c n", p=P)),
                        (rows, a["rows"]), (vecs, a["vecs"]), (par_mask, a["par_mask"]),
                        (ones_h, a["row_masks"]), (gateT, a["gateT"].rearrange("(c p) n -> p c n", p=P)),
                        (tri, a["tri"]), (ones, a["ones"]), (e_idx, a["e_idx"]), (j_idx, a["j_idx"]),
                    ):
                        sp.dma_start(dst[:] if dst is not ones_h else ones_h[0:4, :], src).then_inc(s_w, 16)
                    sp.dma_start(gates[:, 0:1], a["g_xattn"].rearrange("(a n) -> a n", a=1).partition_broadcast(P)).then_inc(s_w, 16)
                    sp.dma_start(gates[:, 1:2], a["g_ffn"].rearrange("(a n) -> a n", a=1).partition_broadcast(P)).then_inc(s_w, 16)

            sp.wait_ge(s_zero, 3)
            zeros = zero_row[:].unsqueeze(1).broadcast_to([P, NE, D])
            sp.dma_start(xs.rearrange("(t p) d -> p t d", p=P), zeros).then_inc(s_zf, 16)

            def load_y(i, b):
                if real(i):
                    ge(sp, s_y, i - 1)
                    src = a["ctxT"][:, bass.ts(i, P)] if not isinstance(i, int) else a["ctxT"][:, i * P:(i + 1) * P]
                    sp.dma_start(y_in[:, b, :], src).then_inc(s_yl[b], 16)

            over_tiles(sp, load_y)

            for n, (src, _) in enumerate(STAGED):
                ge(sp, s_split, 2 * (n - 1))
                sp.dma_start(staged(n, src.shape), src).then_inc(s_ws[n % 2], 16)

            def load_rows(j, b):
                if real(j, NE):
                    ge(sp, ffn["ex"]["xt"], j - 3)
                    sp.dma_start(rows_in[:, b, :], row_tile(xs, j)).then_inc(s_xs[b], 16)

            def store_rows(j, b):
                if real(j, NE):
                    sp.wait_ge(ffn["ex"]["yd"], j + 1)
                    sp.dma_start(row_tile(ys, j), y_sb[:, b % 2, :]).then_inc(s_ys[b % 2], 16)

            def expert_io(i, b):
                load_rows(i + 2 if isinstance(i, int) else i + 2, (b + 2) % 4)
                if real(i - 1, NE):
                    store_rows(i - 1, (b - 1) % 4)

            sp.wait_ge(s_sc1[0], NT * 16)
            sp.wait_ge(s_sc1[1], NT * 16)
            load_rows(0, 0)
            load_rows(1, 1)
            over_tiles(sp, expert_io, NE, 4)

            def store_out(i, b):
                if real(i):
                    sp.wait_ge(s_cmb, i + 1)
                    sp.dma_start(row_tile(out, i), g2[:, b, :]).then_inc(s_os[b], 16)

            over_tiles(sp, store_out)
            for n in range(2):
                sp.wait_ge(s_ys[n], NE // 2 * 16)
                sp.wait_ge(s_os[n], NT // 2 * 16)

        N_W = 17 * 16

        @block.gpsimd
        def _(pool):
            pool.memset(ident[:], 0.0).then_inc(s_id, 1)
            pool.wait_ge(s_id, 1)
            pool.affine_select(out=ident[:], in_=ident[:], compare_op=ALU.not_equal, fill=1.0, base=0,
                               pattern=[[-1, P]], channel_multiplier=1).then_inc(s_id, 1)
            pool.memset(zero_row[:], 0.0)
            pool.memset(c15[:], 1.5)
            pool.memset(yM[:], 0.0).then_inc(s_zero, 1)
            pool.memset(yD[:], 0.0).then_inc(s_zero, 1)
            pool.memset(vbd[:], 0.0).then_inc(s_zero, 1)
            pool.wait_ge(s_zero, 3)

            def spread_y(i, b):
                ge(pool, s_yl[b], (i - b) * 8 + 16 if not isinstance(i, int) else (i // 2 + 1) * 16)
                ge(pool, s_proj, i - 1)
                settle(pool)
                yi = y_in[:, b, :].rearrange("p (s k) -> p s k", s=2)
                pool.tensor_scalar(yM[:, b, :, 0:NM], yi[:, :, 0:NM], 1.0, None, ALU.mult).then_inc(s_zero, 1)
                pool.tensor_copy(yD[:, b, :, NM:NK], yi[:, :, NM:NK]).then_inc(s_y, 1)

            def step(i, b):
                if real(i + 1) :
                    spread_y(i + 1, 1 - b)
                if real(i):
                    pool.wait_ge(s_var, i + 1)
                    y0 = seed[:, b, :].bitcast(F32)
                    chain = i * 12
                    for n in range(3):
                        src = y0 if n == 0 else ya[:, b, :]
                        if n:
                            pool.wait_ge(s_nw, chain + 4 * n)
                        pool.tensor_tensor(yt[:, b, :], src, src, ALU.mult).then_inc(s_nw, 1)
                        pool.wait_ge(s_nw, chain + 4 * n + 1)
                        pool.tensor_tensor(yt[:, b, :], yt[:, b, :], hv[:, b, :], ALU.mult).then_inc(s_nw, 1)
                        pool.wait_ge(s_nw, chain + 4 * n + 2)
                        pool.tensor_tensor(yt[:, b, :], yt[:, b, :], c15[:], ALU.add).then_inc(s_nw, 1)
                        pool.wait_ge(s_nw, chain + 4 * n + 3)
                        if n == 0:
                            ge(pool, s_qk, i - 1)
                        last = pool.tensor_tensor(ya[:, b, :], src, yt[:, b, :], ALU.mult)
                        last.then_inc(s_nw, 1)
                    pool.wait_ge(s_nw, chain + 12)
                    pool.sem_inc(s_rs, 1)
                if real(i - 1):
                    pb_ = 1 - b
                    pool.wait_ge(s_rd, i)
                    for n, (k0, k1) in enumerate(((0, NM), (NM, NK))):
                        p = S[:, pb_, :, :, k0:k1].rearrange("p g c k -> p (g c) k")
                        r = den[:, pb_, n, :].unsqueeze(2).broadcast_to([P, H, k1 - k0])
                        pool.tensor_tensor(p, p, r, ALU.mult).then_inc(s_nm, 1)

            spread_y(0, 0)
            over_tiles(pool, step)

            for n, (src, (high, rest)) in enumerate(STAGED):
                w = staged(n, src.shape)
                pool.wait_ge(s_ws[n % 2], (n // 2 + 1) * 16)
                pool.tensor_copy(high, w).then_inc(s_split, 1)
                pool.wait_ge(s_split, 2 * n + 1)
                pool.tensor_tensor(rest, w, high.bitcast(F32), ALU.subtract).then_inc(s_split, 1)

            pool.wait_ge(s_zf, 16)
            pool.wait_ge(s_pos, 1)

            def places(i, b):
                for n, pos in enumerate((pos1, pos2)):
                    m = pool.tensor_copy(idx[:, b, n:n + 1], pos[:, i:i + 1] if isinstance(i, int) else pos[:, bass.ds(i, 1)])
                m.then_inc(s_idx, 1)
                return [bass.IndirectOffsetOnAxis(ap=idx[:, b, n:n + 1], axis=0) for n in range(2)]

            def scatter(i, b):
                if real(i):
                    ge(pool, s_sc1[b], (i - b) * 16 if not isinstance(i, int) else i // 2 * 32)
                    settle(pool)
                    to = places(i, b)
                    pool.wait_ge(s_idx, i + 1)
                    pool.wait_ge(ffn["sh"]["x"], i + 1)
                    settle(pool)
                    for n in range(2):
                        pool.indirect_dma_start(xs, to[n], x2[:, b, :], None).then_inc(s_sc1[b], 16)

            over_tiles(pool, scatter)

            pool.wait_ge(s_ys[0], NE // 2 * 16)
            pool.wait_ge(s_ys[1], NE // 2 * 16)

            def gather(i, b):
                if real(i):
                    ge(pool, s_os[b], (i - b) * 8 if not isinstance(i, int) else i // 2 * 16)
                    settle(pool)
                    of = places(i, b)
                    pool.wait_ge(s_idx, NT + i + 1)
                    settle(pool)
                    for n, dst in enumerate((g1, g2)):
                        pool.indirect_dma_start(dst[:, b, :], None, ys, of[n]).then_inc(s_g[b], 16)

            over_tiles(pool, gather)

        @block.scalar
        def _(act):
            act.wait_ge(s_st, 2)
            act.activation(rstd1[:], rstd1[:], ACT.Sqrt).then_inc(s_rt, 1)
            act.wait_ge(s_w, N_W)
            act.activation(tg[:], gates[:], ACT.Tanh).then_inc(s_tg, 1)
            act.wait_ge(s_cen, 1)

            def evac_xnT(i, b):
                act.wait_ge(s_tx, i + 1)
                act.activation(xnT[:, b, :, :], p_x.rearrange("p (c n) -> p c n", c=DC), ACT.Copy).then_inc(s_xe, 1)

            def step(i, b):
                o = 1 - b
                if real(i):
                    act.wait_ge(s_proj, i + 1)
                    ge(act, s_vr, i - 1)
                    act.activation(sq[:, b, :], pQK[:], ACT.Square).then_inc(s_sq, 1)
                    ge(act, s_pv, i - 1)
                    for s in range(2):
                        for par in range(2):
                            pairs = p_v.rearrange("p (j h d) -> p j h d", h=2, d=HD)
                            m = act.activation(vbd[64 * par:64 * par + 64, b, s, :, par, :],
                                               pairs[64 * s:64 * s + 64, :, par, :], ACT.Copy)
                    m.then_inc(s_vev, 1)
                if real(i + 1):
                    evac_xnT(i + 1, o)
                if real(i - 1):
                    act.wait_ge(s_pt, i)
                    act.activation(PT[:, o].rearrange("p g c n -> p g (c n)"), p_pt, ACT.Copy).then_inc(s_pe, 1)
                if real(i):
                    act.wait_ge(s_tq, i + 1)
                    act.activation(qT[:, b].rearrange("p c n -> p (c n)"), pT[:, 0].rearrange("p c n -> p (c n)"), ACT.Identity,
                                   scale=vecs[:, 0:1], bias=vecs[:, 1:2])
                    for par in range(2):
                        for n, (k0, k1) in enumerate(((0, NM), (NM, NK))):
                            m = act.activation(
                                kT[:, b, :, par, :, k0:k1],
                                pT[:, 1].rearrange("p c (s k) -> p c s k", s=2)[:, :, :, k0:k1],
                                ACT.Identity, scale=kvec[:, par, 2 * n:2 * n + 1], bias=kvec[:, par, 2 * n + 1:2 * n + 2])
                    m.then_inc(s_qe, 1)
                if real(i - 1):
                    act.wait_ge(s_pv, i)
                    act.activation(cT[:, o], p_c, ACT.Copy).then_inc(s_ce, 1)
                if real(i):
                    act.wait_ge(s_mx, 2 * (i + 1))
                    act.activation(S[:, b], S[:, b], ACT.Exp, scale=SCALE).then_inc(s_ex, 1)

            evac_xnT(0, 0)
            over_tiles(act, step)

            act.wait_ge(s_v2, 1)
            act.activation(rstd2[:], rstd2[:], ACT.Sqrt).then_inc(s_rt2, 1)

            def evac_x2T(i, b):
                if real(i):
                    act.wait_ge(s_t2, i + 1)
                    ge(act, s_lg, i - 1)
                    act.activation(x2T[:, b].rearrange("p c n -> p (c n)"), bank[b][:, 0:D], ACT.Copy).then_inc(s_e2, 1)

            over_tiles(act, evac_x2T)
            act.wait_ge(s_rx, 1)
            act.activation(lg, lg, ACT.Exp).then_inc(s_re, 1)
            ffn_act(act, "sh", NT)
            ffn_act(act, "ex", NE)

        @block.tensor
        def _(pe):
            def xnT_of(i, b):
                pe.wait_ge(s_xn, i + 1)
                ge(pe, s_qe, i - 1)
                for c in range(DC):
                    m = pe.transpose(p_x[:, c * P:(c + 1) * P], xn[:, b, c * P:(c + 1) * P], ident[:])
                m.then_inc(s_tx, 1)

            def project(i, b):
                pe.wait_ge(s_xe, i + 1)
                pe.wait_ge(s_y, i + 1)
                ge(pe, s_qk, i)
                ge(pe, s_vev, i)
                for c in range(DC):
                    pe.matmul(pQK[:, 0:D], xnT[:, b, c, :], wq[:, c, :], start=(c == 0), stop=False)
                pe.matmul(pQK[:, 0:D], ones_h[2:4, :] if False else ones_h[0:1, :], rows[0:1, 0:D], start=False, stop=True)
                ym = yM[:, b].rearrange("p s k -> p (s k)")
                yd = yD[:, b].rearrange("p s k -> p (s k)")
                pe.matmul(pQK[:, D:2 * D], ym, wkm[:], start=True, stop=False)
                pe.matmul(pQK[:, D:2 * D], yd, wkd[:], start=False, stop=False)
                pe.matmul(pQK[:, D:2 * D], ones_h[0:3, :], rows[0:3, D:2 * D], start=False, stop=True)
                pe.matmul(p_v, ym, wvm[:], start=True, stop=False)
                pe.matmul(p_v, yd, wvd[:], start=False, stop=False)
                pe.matmul(p_v, ones_h[0:3, :], rows[0:3, 2 * D:3 * D], start=False, stop=True).then_inc(s_proj, 1)

            def step(i, b):
                o = 1 - b
                if real(i):
                    project(i, b)
                if real(i + 1):
                    xnT_of(i + 1, o)
                if real(i - 1):
                    pe.wait_ge(s_nm, 2 * i)
                    ge(pe, s_pe, i - 1)
                    for g in range(G):
                        for c in range(DC):
                            m = pe.transpose(p_pt[:, g, c * P:(c + 1) * P],
                                             S[:, o, g, 2 * c:2 * c + 2, :].rearrange("p h k -> p (h k)"), ident[:])
                    m.then_inc(s_pt, 1)
                if real(i):
                    pe.wait_ge(s_qk, i + 1)
                    if real(i + 1):
                        pe.wait_ge(s_xe, i + 2)
                    for n in range(2):
                        for c in range(DC):
                            m = pe.transpose(pT[:, n, c, :], qk[:, b, n * D + c * P:n * D + (c + 1) * P], ident[:])
                    m.then_inc(s_tq, 1)
                if real(i - 1):
                    pe.wait_ge(s_pe, i)
                    pe.wait_ge(s_vev, i)
                    ge(pe, s_res, i - 1)
                    for s in range(2):
                        for c in range(DC):
                            for g in range(G):
                                j = G * c + g
                                m = pe.matmul(p_c[32 * g:32 * g + 32, c, 64 * s:64 * s + 64],
                                              vbd[:, o, s, j].rearrange("p h d -> p (h d)"), PT[:, o, g, c, 64 * s:64 * s + 64],
                                              start=True, stop=True)
                    m.then_inc(s_pv, 1)
                if real(i):
                    pe.wait_ge(s_qe, i + 1)
                    ge(pe, s_mx, 2 * i)
                    for c in range(DC):
                        for s in range(2):
                            for g in range(G):
                                m = pe.matmul(p_sc[64 * s:64 * s + 64, g, c * P:(c + 1) * P],
                                              qT[32 * g:32 * g + 32, b, c, 64 * s:64 * s + 64],
                                              kT[32 * g:32 * g + 32, b, c, :, s, :], start=True, stop=True)
                    m.then_inc(s_sc, 1)
                if real(i - 1):
                    pe.wait_ge(s_ce, i)
                    for c in range(DC):
                        pe.matmul(p_o, cT[:, o, c, :], wo[:, c, :], start=(c == 0), stop=False)
                    pe.matmul(p_o, ones_h[0:1, :], rows[0:1, 3 * D:4 * D], start=False, stop=True).then_inc(s_wo, 1)

            pe.wait_ge(s_id, 2)
            xnT_of(0, 0)
            pe.wait_ge(s_cen, 1)
            over_tiles(pe, step)

            def logits(i, b):
                if real(i):
                    pe.wait_ge(s_n2, i + 1)
                    ge(pe, s_e2, i - 1)
                    for c in range(DC):
                        m = pe.transpose(bank[b][:, c * P:(c + 1) * P], x2[:, b, c * P:(c + 1) * P], ident[:])
                    m.then_inc(s_t2, 1)
                if real(i - 1):
                    o = 1 - b
                    pe.wait_ge(s_e2, i)
                    cols = slice((i - 1) * E, i * E) if isinstance(i, int) else bass.ds((i - 1) * E, E)
                    for c in range(DC):
                        m = pe.matmul(bank[7][:, cols], x2T[:, o, c, :], gateT[:, c, :], start=(c == 0), stop=(c == DC - 1))
                    m.then_inc(s_lg, 1)

            over_tiles(pe, logits)
            pe.wait_ge(s_oh, 1)
            flat = both.rearrange("p t e -> p (t e)")
            pe.matmul(bank[6][:, 0:NT * E], tri[:], flat, start=True, stop=True)
            pe.matmul(bank[5][:, 0:NT * E], ones[:], flat, start=True, stop=True).then_inc(s_cnt, 1)
            pe.wait_ge(s_pos, 1)
            pe.wait_ge(s_split, 2 * len(STAGED))
            ffn_pe(pe, "sh", NT)
            ffn_pe(pe, "ex", NE)

        @block.vector
        def _(dve):
            for n in range(4):
                dve.wait_ge(s_x[n], 16)
                for t in range(n * NT // 4, (n + 1) * NT // 4):
                    m = dve.bn_stats(st1[:, t, :], X[:, t, :])
            m.then_inc(s_st, 1)
            dve.wait_ge(s_st, 1)
            for t in range(NT):
                m = dve.bn_aggr(mv1[:, t, :], st1[:, t, :])
            m.then_inc(s_c, 1)
            dve.wait_ge(s_c, 1)
            dve.tensor_scalar(rstd1[:], mv1[:, :, 1], 1e-5, None, ALU.add).then_inc(s_st, 1)
            dve.wait_ge(s_w, N_W)
            cases = [(wq[:, 0, :], csum[:, 0, :]), (wq[:, 1, :], csum[:, 1, :]), (wkm[:], csum[:, 2, :]),
                     (wkd[:], csum[:, 3, :]), (rows[:, 0:2 * D], bsum[:])]
            for w, s in cases:
                dve.tensor_reduce(s, heads(w), AX.X, ALU.add).then_inc(s_c, 1)
            dve.wait_ge(s_c, 6)
            dve.tensor_scalar(csum[:], csum[:], 1.0 / HD, None, ALU.mult).then_inc(s_c, 1)
            dve.tensor_scalar(bsum[:], bsum[:], 1.0 / HD, None, ALU.mult).then_inc(s_c, 1)
            dve.wait_ge(s_c, 8)
            for w, s in cases:
                n = s.shape[1]
                dve.tensor_tensor(heads(w), heads(w), s.unsqueeze(2).broadcast_to([w.shape[0], n, HD]), ALU.subtract)
            for par in range(2):
                m = dve.tensor_scalar(kvec[:, par, :], vecs[:, 2:6], par_mask[:, par:par + 1], None, ALU.mult)
            m.then_inc(s_cen, 1)
            dve.wait_ge(s_rt, 1)
            dve.reciprocal(rstd1[:], rstd1[:]).then_inc(s_r1, 1)
            dve.wait_ge(s_r1, 1)
            dve.wait_ge(s_tg, 1)
            dve.wait_ge(s_zero, 3)

            def norm_x(i, b):
                ge(dve, s_tx, i - 1)
                dve.tensor_scalar(xn[:, b, :], X[:, i, :], mv1[:, i, 0:1], rstd1[:, bass.ds(i, 1)] if not isinstance(i, int) else rstd1[:, i:i + 1],
                                  ALU.subtract, ALU.mult).then_inc(s_xn, 1)

            def step(i, b):
                o = 1 - b
                if real(i):
                    dve.wait_ge(s_sq, i + 1)
                    dve.tensor_reduce(var[:, b, :], heads(sq[:, b, :]), AX.X, ALU.add).then_inc(s_vr, 1)
                    dve.wait_ge(s_vr, i + 1)
                    ge(dve, s_rs, i - 1)
                    dve.tensor_scalar(var[:, b, :], var[:, b, :], 1.0 / HD, 1e-6, ALU.mult, ALU.add).then_inc(s_seed, 1)
                    dve.wait_ge(s_seed, 3 * i + 1)
                    dve.tensor_scalar(hv[:, b, :], var[:, b, :], -0.5, None, ALU.mult).then_inc(s_seed, 1)
                    dve.tensor_scalar(seed[:, b, :], var[:, b, :].bitcast(I32), 1, None, ALU.arith_shift_right).then_inc(s_seed, 1)
                    dve.wait_ge(s_seed, 3 * i + 3)
                    dve.tensor_scalar(seed[:, b, :], seed[:, b, :], -1, RSQRT_SEED, ALU.mult, ALU.add).then_inc(s_var, 1)
                if real(i + 1):
                    norm_x(i + 1, o)
                if real(i - 1):
                    dve.wait_ge(s_ex, i)
                    for n, (k0, k1) in enumerate(((0, NM), (NM, NK))):
                        dve.tensor_reduce(den[:, o, n, :], S[:, o, :, :, k0:k1].rearrange("p g c k -> p (g c) k"), AX.X,
                                          ALU.add).then_inc(s_sum, 1)
                    dve.wait_ge(s_sum, 2 * i)
                    dve.reciprocal(den[:, o], den[:, o]).then_inc(s_rd, 1)
                if real(i):
                    dve.wait_ge(s_rs, i + 1)
                    ge(dve, s_tq, i - 1)
                    dve.tensor_tensor(heads(qk[:, b, :]), heads(pQK[:]),
                                      ya[:, b, :].unsqueeze(2).broadcast_to([P, 2 * H, HD]), ALU.mult).then_inc(s_qk, 1)
                if real(i - 2):
                    t = i - 2
                    dve.wait_ge(s_wo, i - 1)
                    dve.scalar_tensor_tensor(out=xm[:, b, :], in0=p_o, scalar=tg[:, 0:1], in1=X[:, t, :],
                                             op0=ALU.mult, op1=ALU.add).then_inc(s_res, 1)
                    dve.wait_ge(s_res, i - 1)
                    dve.bn_stats(st2[:, b, :], xm[:, b, :]).then_inc(s_b2, 1)
                    dve.wait_ge(s_b2, 2 * i - 3)
                    dve.tensor_scalar(X[:, t, :], xm[:, b, :], 1.0, None, ALU.mult)
                    dve.bn_aggr(mvr[:, b, :], st2[:, b, :]).then_inc(s_b2, 1)
                    dve.wait_ge(s_b2, 2 * i - 2)
                    dve.tensor_scalar(mv2[:, t, :], mvr[:, b, :], 1.0, None, ALU.mult).then_inc(s_l2, 1)
                if real(i):
                    dve.wait_ge(s_sc, i + 1)
                    ge(dve, s_pt, i - 1)
                    sc = p_sc.rearrange("p g (c k) -> p g c k", k=NK)
                    for n, (k0, k1) in enumerate(((0, NM), (NM, NK))):
                        dve.tensor_reduce(mx[:, b, n], sc[:, :, :, k0:k1], AX.X, ALU.max).then_inc(s_max, 1)
                    dve.wait_ge(s_max, 2 * (i + 1))
                    for n, (k0, k1) in enumerate(((0, NM), (NM, NK))):
                        dve.tensor_tensor(S[:, b, :, :, k0:k1], sc[:, :, :, k0:k1],
                                          mx[:, b, n].unsqueeze(3).broadcast_to([P, G, 4, k1 - k0]), ALU.subtract).then_inc(s_mx, 1)

            norm_x(0, 0)
            over_tiles(dve, step)

            dve.wait_ge(s_l2, NT)
            dve.tensor_scalar(rstd2[:], mv2[:, :, 1], 1e-5, None, ALU.add).then_inc(s_v2, 1)
            dve.wait_ge(s_rt2, 1)
            dve.reciprocal(rstd2[:], rstd2[:]).then_inc(s_r2, 1)
            dve.wait_ge(s_r2, 1)

            def norm_2(i, b):
                return dve.tensor_scalar(x2[:, b, :], X[:, i, :], mv2[:, i, 0:1],
                                         rstd2[:, i:i + 1] if isinstance(i, int) else rstd2[:, bass.ds(i, 1)],
                                         ALU.subtract, ALU.mult)

            def x2_step(i, b):
                if real(i):
                    ge(dve, s_t2, i - 1)
                    norm_2(i, b).then_inc(s_n2, 1)

            over_tiles(dve, x2_step)
            route(dve)

            def x2_again(i, b):
                ge(dve, ffn["sh"]["xt"], i - 1)
                ge(dve, s_sc1[b], (i - b) * 16 if not isinstance(i, int) else i // 2 * 32)
                norm_2(i, b).then_inc(ffn["sh"]["x"], 1)

            ffn_dve(dve, "sh", NT, x2_again)
            ffn_dve(dve, "ex", NE, None)
            dve.tensor_scalar(w1, w1, tg[:, 1:2], None, ALU.mult).then_inc(s_o1, 1)
            dve.tensor_scalar(w2, w2, tg[:, 1:2], None, ALU.mult).then_inc(s_o1, 1)
            dve.wait_ge(s_o1, 2)

            def combine(i, b):
                if real(i):
                    dve.wait_ge(s_g[b], (i - b) * 16 + 32 if not isinstance(i, int) else (i // 2 + 1) * 32)
                    wa, wb = (w[:, i:i + 1] if isinstance(i, int) else w[:, bass.ds(i, 1)] for w in (w1, w2))
                    dve.scalar_tensor_tensor(out=g1[:, b, :], in0=g1[:, b, :], scalar=wa, in1=X[:, i, :],
                                             op0=ALU.mult, op1=ALU.add).then_inc(s_o1, 1)
                    dve.wait_ge(s_o1, i + 3)
                    dve.scalar_tensor_tensor(out=g2[:, b, :], in0=g2[:, b, :], scalar=wb, in1=g1[:, b, :],
                                             op0=ALU.mult, op1=ALU.add).then_inc(s_cmb, 1)

            over_tiles(dve, combine)


def layout(np, i):
    f = lambda n: np.asarray(i[n])
    T, D = 4096, 256
    HD = 16
    wkv = np.concatenate([f("L0_xattn_Wk"), f("L0_xattn_Wv")], axis=1).reshape(128, 16, 2, HD)
    bkv = np.concatenate([f("L0_xattn_bk"), f("L0_xattn_bv")]).reshape(16, 2, HD)
    wd = f("L0_xattn_Wkv_dca").reshape(128, 2, 16, HD)
    bd = f("L0_xattn_bkv_dca").reshape(2, 16, HD)
    flat = lambda w: np.ascontiguousarray(w.reshape(w.shape[0], -1))
    rows = np.zeros((4, 4, D), np.float32)
    rows[0, 0] = f("L0_xattn_bq")
    rows[1, 1], rows[2, 1] = bkv[:, 0].ravel(), bd[0].ravel()
    rows[1, 2], rows[2, 2] = bkv[:, 1].ravel(), bd[1].ravel()
    rows[0, 3] = f("L0_xattn_bo")
    masks = np.zeros((4, 2, 64), np.float32)
    masks[0] = 1
    masks[1, :, :48] = 1
    masks[2, :, 48:] = 1
    vec = [np.tile(f("L0_xattn_" + n), 8) for n in ("qn_w", "qn_b", "kn_w", "kn_b", "kn_dca_w", "kn_dca_b")]
    par = (np.arange(128) // HD % 2)
    k_first = lambda w: np.ascontiguousarray(w.reshape(w.shape[0], w.shape[1], 2, 128).transpose(0, 3, 2, 1))
    return {
        "x": f("x").reshape(T, D), "ctxT": np.ascontiguousarray(f("ctx_1024").reshape(T, 128).T),
        "wq": f("L0_xattn_Wq"), "wkm": flat(wkv[:, :, 0]), "wvm": flat(wkv[:, :, 1]),
        "wkd": flat(wd[:, 0]), "wvd": flat(wd[:, 1]), "wo": f("L0_xattn_Wo"),
        "rows": rows.reshape(4, 4 * D), "row_masks": masks.reshape(4, 128),
        "vecs": np.stack(vec, axis=1), "par_mask": np.stack([1 - par, par], 1).astype(np.float32),
        "g_xattn": f("g_xattn"), "g_ffn": f("g_ffn"),
        "gateT": np.ascontiguousarray(f("L0_ffn_gate_weight").T),
        "w_gu": k_first(np.concatenate([f("L0_ffn_w_gate"), f("L0_ffn_w_up")], axis=1)),
        "w_dn": np.ascontiguousarray(f("L0_ffn_w_down").transpose(0, 2, 1)),
        "s_gu": np.ascontiguousarray(np.concatenate([f("L0_ffn_sw_gate"), f("L0_ffn_sw_up")], axis=0).T.reshape(2, 128, -1)),
        "s_dn": np.ascontiguousarray(f("L0_ffn_sw_down").T),
        "tri": np.triu(np.ones((128, 128), np.float32), 1), "ones": np.ones((128, 128), np.float32),
        "e_idx": np.tile(np.arange(8, dtype=np.float32), (128, 1)),
        "j_idx": np.tile(np.arange(72, dtype=np.float32), (128, 1)),
    }


def kernel(**inputs):
    import numpy as _np
    import concourse.bacc as _bacc
    from concourse.bass_utils import run_bass_kernel_spmd as _run

    nc = _bacc.Bacc("TRN2", target_bir_lowering=False, num_devices=1)
    arrays, aps = {}, {}
    for name, array in layout(_np, inputs).items():
        array = _np.ascontiguousarray(array)
        arrays[f"in_{name}_dram"] = array
        aps[name] = nc.dram_tensor(f"in_{name}_dram", array.shape, mybir.dt.from_np(array.dtype), kind="ExternalInput").ap()
    out = nc.dram_tensor("out_dram", (4096, 256), F32, kind="ExternalOutput").ap()
    gated_cross_attention_and_moe(nc, aps, out)
    r = _run(nc, [arrays], core_ids=[0])
    return r.results[0]["out_dram"].reshape(64, 64, 256)
```

```python
from contextlib import ExitStack

import concourse.bass as bass
from concourse import mybir

ALU = mybir.AluOpType
ACT = mybir.ActivationFunctionType
AX = mybir.AxisListType
F32 = mybir.dt.float32
F32R = mybir.dt.float32r
I32 = mybir.dt.int32
P = 128


def gated_cross_attention_and_moe(nc, a, out):
    T, D = a["x"].shape
    NS = 64
    NQ = T // NS
    NM, ND = 48, 16
    NK = NM + ND
    HD = 16
    H = D // HD
    NT = T // P
    DC = D // P
    G = P // 32
    SCALE = float(HD) ** -0.5
    RSQRT_SEED = 0x5F3759DF
    E = a["gateT"].shape[1]
    F = 176
    FS = 2 * F
    NE = (2 * T + E * (P - 1)) // P
    NE += -NE % 4
    CUTS = {"sh": [(k, min(k + P, FS)) for k in range(0, FS, P)], "ex": [(k, min(k + P, F)) for k in range(0, F, P)]}

    with ExitStack() as ctx:
        def sb(name, shape, dt=F32):
            return ctx.enter_context(nc.sbuf_tensor(name, shape, dt))

        def pb(name, shape, dt=F32):
            return ctx.enter_context(nc.psum_tensor(name, shape, dt))

        def sem(name):
            return ctx.enter_context(nc.semaphore(name))

        ident = sb("ident", [P, P])
        proj = [sb(f"proj_{n}", [P, 8, D], F32R) for n in "hl"]
        WQ, WKM, WVM, WKD, WVD, WO = 0, 2, 3, 4, 5, 6
        rows_r = sb("rows_r", [64, 4 * D], F32R)
        masks_r = sb("masks_r", [64, P], F32R)
        vecs = sb("vecs", [P, 6])
        gates = sb("gates", [P, 2])
        tg = sb("tg", [P, 2])
        par_mask = sb("par_mask", [P, 2])
        kvec = sb("kvec", [P, 2, 4])
        csum = sb("csum", [P, 5, H])
        bsum = sb("bsum", [4, 2 * H])
        gateT = sb("gateT", [P, DC, E])
        tri = sb("tri", [P, P])
        ones = sb("ones", [P, P])
        e_idx = sb("e_idx", [P, E])
        j_idx = sb("j_idx", [P, NE])
        WALL = a["w_all"].shape[1]
        PIECE = 384
        NPIECE = WALL // PIECE
        w_all = [sb(f"w_all_{n}", [P, WALL], F32R) for n in "hl"]
        at = 0
        views = []
        for chunks, width in ((DC, E * 2 * F), (2, E * D), (DC, 2 * FS), (3, D)):
            views.append([w[:, at:at + chunks * width].rearrange("p (c n) -> p c n", c=chunks) for w in w_all])
            at += chunks * width
        gu, dn, sgu, sdn = views
        assert at == WALL and WALL % PIECE == 0 and NPIECE <= NT
        yTs = [sb(f"yT_{n}", [P, 2, 2, 2, NK], F32R) for n in "hl"]
        xTs = [sb(f"xT_{n}", [P, 2, DC, P], F32R) for n in "hl"]
        hTs = [sb(f"hT_{n}", [P, 2, 3, P], F32R) for n in "hl"]
        idx = sb("idx", [P, 4, 2], mybir.dt.uint32)
        c15 = sb("c15", [P, 2 * H])
        zero_row = sb("zero_row", [P, D])
        X = sb("X", [P, NT, D])
        st1 = sb("st1", [P, NT, 6])
        mv1 = sb("mv1", [P, NT, 2])
        rstd1 = sb("rstd1", [P, NT])
        rstd2 = sb("rstd2", [P, NT])
        st2 = sb("st2", [P, 2, 6])
        mvr = sb("mvr", [P, 2, 2])
        mv2 = sb("mv2", [P, NT, 2])
        ARENA = 10 * 1024
        arena = sb("arena", [P, ARENA])
        used = [0]

        def take(*shape, dt=F32):
            n = 1
            for d in shape:
                n *= d
            at, used[0] = used[0], used[0] + n
            assert used[0] <= ARENA
            ap = arena[:, at:at + n]
            if dt != F32:
                ap = ap.bitcast(dt)
            names = "abcde"[:len(shape)]
            return ap.rearrange("p (" + " ".join(names) + ") -> p " + " ".join(names),
                                **dict(zip(names, shape))) if len(shape) > 1 else ap

        y_in = take(2, P)
        stage = take(2, PIECE)
        xn = take(2, D)
        sq = take(2 * D)
        var = take(2, 2 * H)
        hv = take(2, 2 * H)
        seed = take(2, 2 * H, dt=I32)
        ya = take(2, 2 * H)
        yt = take(2, 2 * H)
        qk = take(2 * D)
        qT = take(2, DC, P)
        kT = take(2, DC * 2, 2, NK).rearrange("p b (c h) s k -> p b c h s k", c=DC)
        vbd = take(4, 2, H // 2, 2 * HD).rearrange("p b s j (h d) -> p b s j h d", h=2)
        S = take(2, G, 4, NK)
        w_in = S.rearrange("p b g c k -> p (b g c k)").rearrange("p (c n) -> p c n", c=8)
        mx = take(2, 2, G, 4)
        den = take(2, 2, H)
        PT = take(G, DC, P)
        early = PT.rearrange("p g c n -> p (g c n)")
        xm = take(2, D)
        rows = early[0:4, 0:4 * D]
        row_masks = xm.rearrange("p b d -> p (b d)")[0:64, 0:P]
        used[0] = 0
        x2 = take(4, D)
        x2T = take(4, DC, P)
        sg = take(2, FS)
        hid = take(2, FS)
        rows_in = take(4, D)
        y_sb = take(4, D)
        g1 = rows_in
        g2 = take(4, D)
        lg = take(NT, E)
        oh1 = take(NT, E)
        oh2 = take(NT, E)
        both = take(NT, E)
        pfx = take(NT, E)
        cumA = take(NT, E)
        cumB = take(NT, E)
        cand = take(NT, E)
        r1 = take(NT)
        r2 = take(NT)
        w1 = take(NT)
        w2 = take(NT)
        wsum = take(NT)
        pos1f = take(NT)
        pos2f = take(NT)
        pos1 = take(NT, dt=I32)
        pos2 = take(NT, dt=I32)
        tiles_f = take(E)
        tiles_i = take(E, dt=I32)
        endA = take(E)
        endB = take(E)
        start = take(E)
        ge_end = take(NE, E)
        te_f = take(NE)
        te = take(NE, dt=I32)

        pS = pb("pS", [P, G, 512])
        p_sc = pS[:, :, 0:256]
        p_pt = pS[:, :, 256:512]
        pQK = pb("pQK", [P, 512])
        pV = pb("pV", [P, 512])
        p_v = pV[:, 0:D]
        pT = pb("pT", [P, 2, DC, P])
        p_x = pT[:, 0].rearrange("p c n -> p (c n)")
        pCO = pb("pCO", [P, 512])
        p_c = pCO[:, 0:256].rearrange("p (c n) -> p c n", c=DC)
        p_o = pCO[:, 256:512]

        s_w = sem("weights_loaded")
        s_x = [sem(f"x_loaded{n}") for n in range(4)]
        s_id = sem("identity_made")
        s_ws = [sem(f"staged{n}") for n in range(2)]
        s_high, s_split = sem("weights_high"), sem("weights_split")
        s_yz, s_yh = sem("y_zeros"), sem("y_high")
        s_wh, s_in = sem("proj_high"), sem("proj_in")
        s_tidy = sem("proj_ready")
        s_zf = sem("rows_zeroed")
        s_v2, s_rt2, s_r2 = sem("ln2_var"), sem("ln2_roots"), sem("ln2_rstd")
        s_n2, s_t2, s_e2, s_lg = sem("x2_ready"), sem("x2T_in_psum"), sem("x2T_ready"), sem("logits_ready")
        s_rx, s_rs_, s_oh, s_cnt = sem("router_exp_in"), sem("router_step"), sem("choices_ready"), sem("counts_ready")
        s_re, s_pos = sem("router_exp"), sem("positions_ready")
        s_sc1 = [sem(f"rows_scattered{n}") for n in range(4)]
        s_xs = [sem(f"expert_rows_loaded{n}") for n in range(4)]
        s_ys = [sem(f"expert_rows_stored{n}") for n in range(4)]
        s_g = [sem(f"rows_gathered{n}") for n in range(4)]
        s_idx = sem("places_copied")
        s_cmb, s_o1 = sem("combined"), sem("first_added")
        s_os = [sem(f"tile_stored{n}") for n in range(4)]
        ffn = {k: {n: sem(f"{k}_{n}") for n in
                   ("x", "xt", "xh", "xl", "gu", "silu", "h", "ht", "hh", "hl", "y", "yd")} for k in ("sh", "ex")}
        s_yl = [sem(f"y_loaded{n}") for n in range(2)]
        s_y = sem("y_spread")
        s_cen = sem("weights_centred")
        s_c = sem("centring_step")
        s_zero = sem("zeros_written")
        s_st = sem("ln1_stats")
        s_rt = sem("ln1_roots")
        s_r1 = sem("ln1_rstd")
        s_tg = sem("gates_ready")
        s_xn, s_tx, s_xh, s_xl = sem("xn_ready"), sem("xnT_in_psum"), sem("xnT_high"), sem("xnT_rest")
        s_pqk, s_proj, s_sq, s_vev = sem("qk_projected"), sem("v_projected"), sem("squared"), sem("v_ready")
        s_vr, s_seed, s_var = sem("var_summed"), sem("seed_shifted"), sem("seed_ready")
        s_nw, s_rs = sem("newton_step"), sem("rstd_ready")
        s_qk, s_tq, s_qe = sem("qk_normed"), sem("qkT_in_psum"), sem("qkT_ready")
        s_sc, s_max, s_mx = sem("scores_ready"), sem("max_ready"), sem("max_subtracted")
        s_ex, s_sum, s_rd = sem("exp_ready"), sem("sums_ready"), sem("reciprocal_ready")
        s_nm, s_pt, s_pe = sem("probs_ready"), sem("probsT_in_psum"), sem("probsT_ready")
        s_pv, s_ch, s_cl, s_wo = sem("ctxT_in_psum"), sem("ctxT_high"), sem("ctxT_rest"), sem("attn_out")
        s_res, s_b2, s_l2 = sem("residual_added"), sem("ln2_bn"), sem("ln2_stats")
        s_out = sem("out_written")

        s_passed = {nc.gpsimd: sem("pool_passed"), nc.tensor: sem("pe_passed"), nc.scalar: sem("act_passed")}

        block = ctx.enter_context(nc.Block())

        def ge(eng, s, value):
            if not isinstance(value, int) or value > 0:
                eng.wait_ge(s, value)

        def settle(eng):
            eng.sem_inc(s_passed[eng], 1)

        def over_tiles(eng, step, n=NT, unroll=2, low=0, ahead=2):
            first = 4
            rounds = (n - ahead - first) // unroll
            for i in range(low, first):
                step(i, i % unroll)
            with eng.Fori(first // unroll, first // unroll + rounds) as r:
                for b in range(unroll):
                    step(r * unroll + b, b)
            for i in range(first + rounds * unroll, n + 2):
                step(i, i % unroll)

        def over_attention(eng, step):
            over_tiles(eng, step, NT, 4, -2, 3)

        def passes(t, b, each, ring=4):
            return (t // ring) * each if isinstance(t, int) else (t - b) * (each // ring)

        def at_tile(ap, t, width=1):
            return ap[:, t * width:(t + 1) * width] if isinstance(t, int) else ap[:, bass.ds(t * width, width)]

        def real(t, n=NT):
            return not isinstance(t, int) or 0 <= t < n

        def heads(ap):
            return ap.rearrange("p (h d) -> p h d", d=HD)

        xs = nc.dram_tensor("rows_by_expert", [NE * P, D], F32, kind="Internal").ap()
        ys = nc.dram_tensor("outputs_by_expert", [NE * P, D], F32, kind="Internal").ap()

        def row_tile(dram, t):
            return dram[t * P:(t + 1) * P, :] if isinstance(t, int) else dram[bass.ts(t, P), :]

        bank = [pS[:, 0, :], pS[:, 1, :], pS[:, 2, :], pS[:, 3, :], pQK[:], pV[:],
                pT[:].rearrange("p a c n -> p (a c n)"), pCO[:]]

        def gate_up(k, b):
            if k == "sh":
                return bank[2 * b][:, 0:FS], bank[2 * b + 1][:, 0:FS]
            return bank[2 * b][:, 0:F], bank[2 * b][:, F:2 * F]

        p_xT, p_hT, p_y = bank[4], bank[5], bank[6]

        def ffn_pe(pe, k, n):
            s, cuts = ffn[k], CUTS[k]
            experts = []

            def products(dst, pairs):
                last = len(pairs) - 1
                for m, ((xh, xl), (wh, wl)) in enumerate(pairs):
                    pe.matmul(dst, xh, wl, start=(m == 0), stop=False)
                    pe.matmul(dst, xl, wh, start=False, stop=False)
                    r = pe.matmul(dst, xh, wh, start=False, stop=(m == last))
                return r

            def step(i, b):
                b2, o = b % 2, 1 - b % 2
                if k == "ex" and b == 0 and real(i, n):
                    first = max(i - 1, 0) if isinstance(i, int) else i - 1
                    count = min(i + 4, n) - first if isinstance(i, int) else 5
                    pe.wait_ge(s_pos, 1)
                    settle(pe)
                    tiles = te[0:1, first:first + count] if isinstance(i, int) else te[0:1, bass.ds(first, count)]
                    _, values = nc.values_load_multi_w_load_instructions(
                        tiles, engines=(mybir.EngineType.PE,), min_val=0, max_val=E - 1)
                    experts.clear()
                    experts.extend(values if not isinstance(i, int) or i else [None, *values])

                def transpose_x(t, tb):
                    if k == "sh":
                        pe.wait_ge(s["x"], t + 1)
                        src = x2[:, tb, :]
                    else:
                        pe.wait_ge(s_xs[tb], passes(t, tb, 16) + 16)
                        src = rows_in[:, tb, :]
                    ge(pe, s["xl"], t)
                    for c in range(DC):
                        m = pe.transpose(p_xT[:, c * P:(c + 1) * P], src[:, c * P:(c + 1) * P], ident[:])
                    m.then_inc(s["xt"], 1)

                if isinstance(i, int) and i == 0:
                    transpose_x(0, 0)
                if real(i + 1, n):
                    transpose_x(i + 1, (b + 1) % 4)
                if real(i - 1, n):
                    pe.wait_ge(s["h"], i)
                    ge(pe, s["hl"], i - 1)
                    for m, (k0, k1) in enumerate(cuts):
                        r = pe.transpose(p_hT[0:k1 - k0, m * P:(m + 1) * P], hid[:, o, k0:k1], ident[:])
                    r.then_inc(s["ht"], 1)
                if real(i, n):
                    pe.wait_ge(s["xl"], i + 1)
                    ge(pe, s["h"], i - 1)
                    x = [(xTs[0][:, b2, c, :], xTs[1][:, b2, c, :]) for c in range(DC)]
                    if k == "sh":
                        for m, dst in enumerate(gate_up(k, b2)):
                            r = products(dst, [(x[c], [w[:, c, m * FS:(m + 1) * FS] for w in sgu]) for c in range(DC)])
                    else:
                        e = experts[b + 1]
                        cols = bass.ds(e * (2 * F), 2 * F)
                        r = products(bank[2 * b2][:, 0:2 * F], [(x[c], [w[:, c, cols] for w in gu]) for c in range(DC)])
                    r.then_inc(s["gu"], 1)
                if real(i - 1, n):
                    pe.wait_ge(s["hl"], i)
                    ge(pe, s["yd"], i - 1)
                    h = [(hTs[0][0:k1 - k0, o, m, :], hTs[1][0:k1 - k0, o, m, :]) for m, (k0, k1) in enumerate(cuts)]
                    if k == "sh":
                        w = [[w[0:k1 - k0, m, :] for w in sdn] for m, (k0, k1) in enumerate(cuts)]
                    else:
                        e = experts[b] if real(i, n) else experts[-1]
                        w = [[w[0:k1 - k0, m, bass.ds(e * D, D)] for w in dn] for m, (k0, k1) in enumerate(cuts)]
                    products(p_y[:, 0:D], list(zip(h, w))).then_inc(s["y"], 1)

            over_tiles(pe, step, n, 4)

        def ffn_act(act, k, n):
            s, cuts = ffn[k], CUTS[k]

            def high_x(t, b):
                act.wait_ge(s["xt"], t + 1)
                ge(act, s["gu"], t - 1)
                act.activation(xTs[0][:, b].rearrange("p c n -> p (c n)"), p_xT[:, 0:D], ACT.Copy).then_inc(s["xh"], 1)

            def step(i, b):
                e, o = b % 2, 1 - b % 2
                if isinstance(i, int) and i == 0:
                    high_x(0, 0)
                if real(i + 1, n):
                    high_x(i + 1, o)
                if real(i - 1, n):
                    act.wait_ge(s["ht"], i)
                    ge(act, s["y"], i - 2)
                    for m, (k0, k1) in enumerate(cuts):
                        r = act.activation(hTs[0][0:k1 - k0, o, m, :], p_hT[0:k1 - k0, m * P:(m + 1) * P], ACT.Copy)
                    r.then_inc(s["hh"], 1)
                if real(i, n):
                    act.wait_ge(s["gu"], i + 1)
                    ge(act, s["h"], i - 1)
                    act.activation(sg[:, e, 0:cuts[-1][1]], gate_up(k, e)[0], ACT.Silu).then_inc(s["silu"], 1)
                if k == "ex" and real(i - 1, n):
                    act.wait_ge(s["y"], i)
                    r = (b - 1) % 4
                    ge(act, s_ys[r], passes(i - 1, r, 16))
                    act.activation(y_sb[:, r, :], p_y[:, 0:D], ACT.Copy).then_inc(s["yd"], 1)

            over_tiles(act, step, n, 4)

        def ffn_dve(dve, k, n, make_x):
            s, cuts = ffn[k], CUTS[k]

            def rest_x(t, b):
                dve.wait_ge(s["xh"], t + 1)
                ge(dve, s["gu"], t - 1)
                dve.tensor_tensor(xTs[1][:, b].rearrange("p c n -> p (c n)"), p_xT[:, 0:D],
                                  xTs[0][:, b].rearrange("p c n -> p (c n)").bitcast(F32), ALU.subtract).then_inc(s["xl"], 1)

            def step(i, b):
                e, o = b % 2, 1 - b % 2
                if isinstance(i, int) and i == 0:
                    if make_x:
                        for t in range(3):
                            make_x(t, t)
                    rest_x(0, 0)
                if real(i + 1, n):
                    rest_x(i + 1, o)
                if real(i - 1, n):
                    dve.wait_ge(s["hh"], i)
                    ge(dve, s["y"], i - 2)
                    for m, (k0, k1) in enumerate(cuts):
                        r = dve.tensor_tensor(hTs[1][0:k1 - k0, o, m, :], p_hT[0:k1 - k0, m * P:(m + 1) * P],
                                              hTs[0][0:k1 - k0, o, m, :].bitcast(F32), ALU.subtract)
                    r.then_inc(s["hl"], 1)
                if real(i, n):
                    dve.wait_ge(s["silu"], i + 1)
                    ge(dve, s["ht"], i - 1)
                    w = cuts[-1][1]
                    dve.tensor_tensor(hid[:, e, 0:w], sg[:, e, 0:w], gate_up(k, e)[1], ALU.mult).then_inc(s["h"], 1)
                if make_x and real(i + 3, n):
                    make_x(i + 3, (b + 3) % 4)
                if k == "sh" and real(i - 1, n):
                    t = i - 1
                    dve.wait_ge(s["y"], i)
                    dve.scalar_tensor_tensor(out=X[:, t, :], in0=p_y[:, 0:D], scalar=tg[:, 1:2], in1=X[:, t, :],
                                             op0=ALU.mult, op1=ALU.add).then_inc(s["yd"], 1)

            over_tiles(dve, step, n, 4, ahead=3)

        def route(dve):
            count = [0]

            def done(ins):
                count[0] += 1
                ins.then_inc(s_rs_, 1)
                dve.wait_ge(s_rs_, count[0])

            def over_e(v):
                return v.unsqueeze(2).broadcast_to([P, NT, E])

            def over_t(v):
                return v.unsqueeze(1).broadcast_to([P, NT, E])

            dve.wait_ge(s_lg, NT)
            p_lg = bank[7][:, 0:NT * E].rearrange("p (t e) -> p t e", e=E)
            done(dve.tensor_reduce(r1, p_lg, AX.X, ALU.max))
            dve.tensor_tensor(lg, p_lg, over_e(r1), ALU.subtract).then_inc(s_rx, 1)
            dve.wait_ge(s_re, 1)
            done(dve.tensor_reduce(r1, lg, AX.X, ALU.add))
            done(dve.reciprocal(r1, r1))
            done(dve.tensor_tensor(lg, lg, over_e(r1), ALU.mult))
            for w, oh in ((w1, oh1), (w2, oh2)):
                done(dve.tensor_reduce(w, lg, AX.X, ALU.max))
                done(dve.tensor_tensor(cand, lg, over_e(w), ALU.is_lt))
                done(dve.scalar_tensor_tensor(out=cand, in0=cand, scalar=float(E), in1=over_t(e_idx[:]), op0=ALU.mult, op1=ALU.add))
                done(dve.tensor_reduce(r2, cand, AX.X, ALU.min))
                done(dve.tensor_tensor(oh, over_t(e_idx[:]), over_e(r2), ALU.is_equal))
                if w is w1:
                    done(dve.scalar_tensor_tensor(out=lg, in0=oh, scalar=-2.0, in1=lg, op0=ALU.mult, op1=ALU.add))
            dve.tensor_tensor(both, oh1, oh2, ALU.add).then_inc(s_oh, 1)
            done(dve.tensor_tensor(wsum, w1, w2, ALU.add))
            done(dve.tensor_scalar(wsum, wsum, 1e-20, None, ALU.add))
            done(dve.reciprocal(wsum, wsum))
            done(dve.tensor_tensor(w1, w1, wsum, ALU.mult))
            done(dve.tensor_tensor(w2, w2, wsum, ALU.mult))
            dve.wait_ge(s_cnt, 1)
            done(dve.tensor_copy(pfx, bank[6][:, 0:NT * E].rearrange("p (t e) -> p t e", e=E)))
            done(dve.tensor_copy(cumA, bank[5][:, 0:NT * E].rearrange("p (t e) -> p t e", e=E)))
            done(dve.tensor_tensor(pfx, pfx, cumA, ALU.subtract))
            src, dst, d = cumA, cumB, 1
            while d < NT:
                done(dve.tensor_copy(dst[:, 0:d, :], src[:, 0:d, :]))
                done(dve.tensor_tensor(dst[:, d:NT, :], src[:, d:NT, :], src[:, 0:NT - d, :], ALU.add))
                src, dst, d = dst, src, 2 * d
            done(dve.tensor_tensor(pfx, pfx, src, ALU.add))
            done(dve.tensor_scalar(tiles_f, src[:, NT - 1, :], float(P - 1), None, ALU.add))
            done(dve.tensor_copy(tiles_i, tiles_f))
            done(dve.tensor_scalar(tiles_i, tiles_i, 7, None, ALU.arith_shift_right))
            done(dve.tensor_copy(tiles_f, tiles_i))
            done(dve.tensor_copy(endA, tiles_f))
            a_, b_, d = endA, endB, 1
            while d < E:
                done(dve.tensor_copy(b_[:, 0:d], a_[:, 0:d]))
                done(dve.tensor_tensor(b_[:, d:E], a_[:, d:E], a_[:, 0:E - d], ALU.add))
                a_, b_, d = b_, a_, 2 * d
            done(dve.tensor_tensor(start, a_, tiles_f, ALU.subtract))
            done(dve.tensor_scalar(start, start, float(P), None, ALU.mult))
            done(dve.tensor_tensor(pfx, pfx, over_t(start), ALU.add))
            for oh, pf, pos in ((oh1, pos1f, pos1), (oh2, pos2f, pos2)):
                done(dve.tensor_tensor(cand, oh, pfx, ALU.mult))
                done(dve.tensor_reduce(pf, cand, AX.X, ALU.add))
                done(dve.tensor_copy(pos, pf))
            done(dve.tensor_tensor(ge_end, j_idx[:].unsqueeze(2).broadcast_to([P, NE, E]),
                                   a_.unsqueeze(1).broadcast_to([P, NE, E]), ALU.is_ge))
            done(dve.tensor_reduce(te_f, ge_end, AX.X, ALU.add))
            done(dve.tensor_scalar(te_f, te_f, float(E - 1), None, ALU.min))
            dve.tensor_copy(te, te_f).then_inc(s_pos, 1)

        @block.sync
        def _(sp):
            for n in range(4):
                q = NT // 4
                sp.dma_start(X[:, n * q:(n + 1) * q, :],
                             a["x"].rearrange("(t p) d -> p t d", p=P)[:, n * q:(n + 1) * q, :]).then_inc(s_x[n], 16)
                if n == 0:
                    for dst, src in (
                        (w_in[:, WQ:WQ + DC], a["wq"].rearrange("(c p) n -> p c n", p=P)),
                        (w_in[:, WKM:WKM + 4], a["wkv"].rearrange("w p n -> p w n")),
                        (w_in[:, WO:WO + DC], a["wo"].rearrange("(c p) n -> p c n", p=P)),
                        (rows, a["rows"]), (vecs[:], a["vecs"]), (par_mask[:], a["par_mask"]),
                        (row_masks, a["row_masks"]), (gateT[:], a["gateT"].rearrange("(c p) n -> p c n", p=P)),
                        (tri[:], a["tri"]), (ones[:], a["ones"]), (e_idx[:], a["e_idx"]), (j_idx[:], a["j_idx"]),
                    ):
                        sp.dma_start(dst, src).then_inc(s_w, 16)
                    sp.dma_start(gates[:, 0:1], a["g_xattn"].rearrange("(a n) -> a n", a=1).partition_broadcast(P)).then_inc(s_w, 16)
                    sp.dma_start(gates[:, 1:2], a["g_ffn"].rearrange("(a n) -> a n", a=1).partition_broadcast(P)).then_inc(s_w, 16)

            def load_y(t, b):
                if real(t):
                    ge(sp, s_y, t - 1)
                    src = a["ctxT"][:, bass.ts(t, P)] if not isinstance(t, int) else a["ctxT"][:, t * P:(t + 1) * P]
                    sp.dma_start(y_in[:, b, :], src).then_inc(s_yl[b], 16)

            def attention_io(i, b):
                load_y(i + 3, (b + 3) % 2)
                if real(i, NPIECE):
                    ge(sp, s_split, i - 1)
                    sp.dma_start(stage[:, b % 2, :], at_tile(a["w_all"], i, PIECE)).then_inc(s_ws[b % 2], 16)
                if isinstance(i, int) and i == 2:
                    sp.wait_ge(s_zero, 2)
                    zeros = zero_row[:].unsqueeze(1).broadcast_to([P, NE, D])
                    sp.dma_start(xs.rearrange("(t p) d -> p t d", p=P), zeros).then_inc(s_zf, 16)

            load_y(0, 0)
            over_attention(sp, attention_io)

            def load_rows(j, b):
                if real(j, NE):
                    ge(sp, ffn["ex"]["xt"], j - 3)
                    sp.dma_start(rows_in[:, b, :], row_tile(xs, j)).then_inc(s_xs[b], 16)

            def store_rows(j, b):
                if real(j, NE):
                    sp.wait_ge(ffn["ex"]["yd"], j + 1)
                    sp.dma_start(row_tile(ys, j), y_sb[:, b, :]).then_inc(s_ys[b], 16)

            def expert_io(i, b):
                load_rows(i + 3, (b + 3) % 4)
                if real(i - 1, NE):
                    store_rows(i - 1, (b - 1) % 4)

            for done in s_sc1:
                sp.wait_ge(done, NT // 4 * 32)
            for j in range(3):
                load_rows(j, j)
            over_tiles(sp, expert_io, NE, 4, ahead=3)

            def store_out(i, b):
                if real(i):
                    sp.wait_ge(s_cmb, i + 1)
                    sp.dma_start(row_tile(out, i), g2[:, b, :]).then_inc(s_os[b], 16)

            over_tiles(sp, store_out, unroll=4)
            for n in range(4):
                sp.wait_ge(s_ys[n], NE // 4 * 16)
                sp.wait_ge(s_os[n], NT // 4 * 16)

        N_W = 14 * 16

        @block.gpsimd
        def _(pool):
            pool.memset(ident[:], 0.0).then_inc(s_id, 1)
            pool.wait_ge(s_id, 1)
            pool.affine_select(out=ident[:], in_=ident[:], compare_op=ALU.not_equal, fill=1.0, base=0,
                               pattern=[[-1, P]], channel_multiplier=1).then_inc(s_id, 1)
            pool.memset(zero_row[:], 0.0)
            pool.memset(c15[:], 1.5)
            pool.memset(vbd[:], 0.0).then_inc(s_zero, 1)
            pool.memset(yTs[0][:].bitcast(F32), 0.0).then_inc(s_yz, 1)
            pool.memset(yTs[1][:].bitcast(F32), 0.0).then_inc(s_yz, 1)
            pool.memset(rows_r[:].bitcast(F32), 0.0).then_inc(s_zero, 1)
            pool.wait_ge(s_yz, 2)

            def spread_y(t, b):
                ge(pool, s_yl[b], (t - b) * 8 + 16 if not isinstance(t, int) else (t // 2 + 1) * 16)
                ge(pool, s_proj, t - 1)
                settle(pool)
                yi = y_in[:, b, :].rearrange("p (s k) -> p s k", s=2)
                for n, (k0, k1) in enumerate(((0, NM), (NM, NK))):
                    m = pool.tensor_copy(yTs[0][:, b, n, :, k0:k1], yi[:, :, k0:k1])
                m.then_inc(s_yh, 1)
                pool.wait_ge(s_yh, t + 1)
                for n, (k0, k1) in enumerate(((0, NM), (NM, NK))):
                    m = pool.tensor_tensor(yTs[1][:, b, n, :, k0:k1], yi[:, :, k0:k1],
                                           yTs[0][:, b, n, :, k0:k1].bitcast(F32), ALU.subtract)
                m.then_inc(s_y, 1)

            def newton(t, b):
                pool.wait_ge(s_var, t + 1)
                y0 = seed[:, b, :].bitcast(F32)
                chain = t * 12
                for n in range(3):
                    src = y0 if n == 0 else ya[:, b, :]
                    if n:
                        pool.wait_ge(s_nw, chain + 4 * n)
                    pool.tensor_tensor(yt[:, b, :], src, src, ALU.mult).then_inc(s_nw, 1)
                    pool.wait_ge(s_nw, chain + 4 * n + 1)
                    pool.tensor_tensor(yt[:, b, :], yt[:, b, :], hv[:, b, :], ALU.mult).then_inc(s_nw, 1)
                    pool.wait_ge(s_nw, chain + 4 * n + 2)
                    pool.tensor_tensor(yt[:, b, :], yt[:, b, :], c15[:], ALU.add).then_inc(s_nw, 1)
                    pool.wait_ge(s_nw, chain + 4 * n + 3)
                    if n == 0:
                        ge(pool, s_qk, t - 1)
                    pool.tensor_tensor(ya[:, b, :], src, yt[:, b, :], ALU.mult).then_inc(s_nw, 1)
                pool.wait_ge(s_nw, chain + 12)
                pool.sem_inc(s_rs, 1)

            def normalise(t, b):
                pool.wait_ge(s_rd, t + 1)
                for n, (k0, k1) in enumerate(((0, NM), (NM, NK))):
                    p = S[:, b, :, :, k0:k1].rearrange("p g c k -> p (g c) k")
                    r = den[:, b, n, :].unsqueeze(2).broadcast_to([P, H, k1 - k0])
                    pool.tensor_tensor(p, p, r, ALU.mult).then_inc(s_nm, 1)

            def step(i, b):
                even, odd = b % 2, (b + 1) % 2
                if real(i + 1):
                    newton(i + 1, odd)
                if real(i + 2):
                    spread_y(i + 2, even)
                if real(i, NPIECE):
                    pool.wait_ge(s_high, i + 1)
                    settle(pool)
                    pool.tensor_tensor(at_tile(w_all[1], i, PIECE), stage[:, even, :],
                                       at_tile(w_all[0], i, PIECE).bitcast(F32), ALU.subtract).then_inc(s_split, 1)
                if real(i):
                    normalise(i, even)

            over_attention(pool, step)

            pool.wait_ge(s_zf, 16)
            pool.wait_ge(s_pos, 1)


            def places(i, b):
                for n, pos in enumerate((pos1, pos2)):
                    m = pool.tensor_copy(idx[:, b, n:n + 1], pos[:, i:i + 1] if isinstance(i, int) else pos[:, bass.ds(i, 1)])
                m.then_inc(s_idx, 1)
                return [bass.IndirectOffsetOnAxis(ap=idx[:, b, n:n + 1], axis=0) for n in range(2)]

            def scatter(i, b):
                if real(i):
                    ge(pool, s_sc1[b], passes(i, b, 32))
                    settle(pool)
                    to = places(i, b)
                    pool.wait_ge(s_idx, i + 1)
                    pool.wait_ge(ffn["sh"]["x"], i + 1)
                    settle(pool)
                    for n in range(2):
                        pool.indirect_dma_start(xs, to[n], x2[:, b, :], None).then_inc(s_sc1[b], 16)

            over_tiles(pool, scatter, unroll=4)

            for done in s_ys:
                pool.wait_ge(done, NE // 4 * 16)

            def gather(i, b):
                if real(i):
                    ge(pool, s_os[b], passes(i, b, 16))
                    settle(pool)
                    of = places(i, b)
                    pool.wait_ge(s_idx, NT + i + 1)
                    settle(pool)
                    for n, dst in enumerate((g1, g2)):
                        pool.indirect_dma_start(dst[:, b, :], None, ys, of[n]).then_inc(s_g[b], 16)

            over_tiles(pool, gather, unroll=4)

        @block.scalar
        def _(act):
            act.wait_ge(s_st, 2)
            act.activation(rstd1[:], rstd1[:], ACT.Sqrt).then_inc(s_rt, 1)
            act.wait_ge(s_w, N_W)
            act.activation(tg[:], gates[:], ACT.Tanh).then_inc(s_tg, 1)
            act.wait_ge(s_cen, 1)
            act.activation(masks_r[:], row_masks, ACT.Copy)
            act.wait_ge(s_zero, 2)
            act.activation(rows_r[0:4, :], rows, ACT.Copy)
            act.activation(proj[0][:], w_in, ACT.Copy).then_inc(s_wh, 1)

            def step(i, b):
                even, odd = b % 2, (b + 1) % 2
                if real(i + 1):
                    t = i + 1
                    act.wait_ge(s_pqk, t + 1)
                    ge(act, s_vr, t)
                    act.activation(sq, pQK[:], ACT.Square).then_inc(s_sq, 1)
                if real(i + 2):
                    t = i + 2
                    act.wait_ge(s_tx, t + 1)
                    ge(act, s_pqk, t - 1)
                    act.activation(xTs[0][:, even].rearrange("p c n -> p (c n)"), p_x, ACT.Copy).then_inc(s_xh, 1)
                if real(i + 1):
                    t = i + 1
                    act.wait_ge(s_proj, t + 1)
                    ge(act, s_pv, t - 3)
                    pairs = p_v.rearrange("p (j h d) -> p j h d", h=2, d=HD)
                    for s in range(2):
                        for par in range(2):
                            m = act.activation(vbd[64 * par:64 * par + 64, (b + 1) % 4, s, :, par, :],
                                               pairs[64 * s:64 * s + 64, :, par, :], ACT.Copy)
                    m.then_inc(s_vev, 1)
                if real(i, NPIECE):
                    n = (i - even) * 8 + 16 if not isinstance(i, int) else (i // 2 + 1) * 16
                    act.wait_ge(s_ws[even], n)
                    settle(act)
                    act.activation(at_tile(w_all[0], i, PIECE), stage[:, even, :], ACT.Copy).then_inc(s_high, 1)
                if real(i):
                    act.wait_ge(s_mx, 2 * (i + 1))
                    act.activation(S[:, even], S[:, even], ACT.Exp, scale=SCALE).then_inc(s_ex, 1)
                if real(i - 1):
                    t = i - 1
                    act.wait_ge(s_pt, t + 1)
                    ge(act, s_pv, t)
                    act.activation(PT.rearrange("p g c n -> p g (c n)"), p_pt, ACT.Copy).then_inc(s_pe, 1)
                if real(i + 1):
                    t = i + 1
                    act.wait_ge(s_tq, t + 1)
                    ge(act, s_sc, t - 1)
                    act.activation(qT[:, odd].rearrange("p c n -> p (c n)"), pT[:, 0].rearrange("p c n -> p (c n)"),
                                   ACT.Identity, scale=vecs[:, 0:1], bias=vecs[:, 1:2])
                    for par in range(2):
                        for n, (k0, k1) in enumerate(((0, NM), (NM, NK))):
                            m = act.activation(
                                kT[:, odd, :, par, :, k0:k1],
                                pT[:, 1].rearrange("p c (s k) -> p c s k", s=2)[:, :, :, k0:k1],
                                ACT.Identity, scale=kvec[:, par, 2 * n:2 * n + 1], bias=kvec[:, par, 2 * n + 1:2 * n + 2])
                    m.then_inc(s_qe, 1)
                if real(i - 1):
                    t = i - 1
                    act.wait_ge(s_pv, t + 1)
                    ge(act, s_wo, t - 1)
                    act.activation(hTs[0][:, odd, 0:DC], p_c, ACT.Copy).then_inc(s_ch, 1)

            over_attention(act, step)

            act.wait_ge(s_v2, 1)
            act.activation(rstd2[:], rstd2[:], ACT.Sqrt).then_inc(s_rt2, 1)

            def evac_x2T(i, b):
                if real(i):
                    act.wait_ge(s_t2, i + 1)
                    ge(act, s_lg, i - 3)
                    act.activation(x2T[:, b].rearrange("p c n -> p (c n)"), bank[b][:, 0:D], ACT.Copy).then_inc(s_e2, 1)

            over_tiles(act, evac_x2T, unroll=4)
            act.wait_ge(s_rx, 1)
            act.activation(lg, lg, ACT.Exp).then_inc(s_re, 1)
            ffn_act(act, "sh", NT)
            ffn_act(act, "ex", NE)

        @block.tensor
        def _(pe):
            def parts(dst, pairs, bias=None):
                for m, ((xh, xl), (wh, wl)) in enumerate(pairs):
                    pe.matmul(dst, xh, wl, start=(m == 0), stop=False)
                    pe.matmul(dst, xl, wh, start=False, stop=False)
                    pe.matmul(dst, xh, wh, start=False, stop=False)
                return pe.matmul(dst, masks_r[:], rows_r[:, bias * D:(bias + 1) * D], start=False, stop=True)

            def project(t, b):
                pe.wait_ge(s_xl, t + 1)
                pe.wait_ge(s_y, t + 1)
                ge(pe, s_qk, t)
                w = lambda n: [p[:, n, :] for p in proj]
                x = [[p[:, b, c, :] for p in xTs] for c in range(DC)]
                y = [[p[:, b, n].rearrange("p s k -> p (s k)") for p in yTs] for n in range(2)]
                parts(pQK[:, 0:D], [(x[c], w(WQ + c)) for c in range(DC)], 0)
                parts(pQK[:, D:2 * D], [(y[0], w(WKM)), (y[1], w(WKD))], 1).then_inc(s_pqk, 1)

            def project_v(t, b):
                ge(pe, s_vev, t)
                y = [[p[:, b, n].rearrange("p s k -> p (s k)") for p in yTs] for n in range(2)]
                parts(p_v, [(y[n], [p[:, w, :] for p in proj]) for n, w in enumerate((WVM, WVD))], 2).then_inc(s_proj, 1)

            def step(i, b):
                even, odd = b % 2, (b + 1) % 2
                if real(i + 1):
                    project(i + 1, odd)
                if real(i):
                    pe.wait_ge(s_qe, i + 1)
                    ge(pe, s_mx, 2 * i)
                    ge(pe, s_pe, i - 1)
                    for c in range(DC):
                        for s in range(2):
                            for g in range(G):
                                m = pe.matmul(p_sc[64 * s:64 * s + 64, g, c * P:(c + 1) * P],
                                              qT[32 * g:32 * g + 32, even, c, 64 * s:64 * s + 64],
                                              kT[32 * g:32 * g + 32, even, c, :, s, :], start=True, stop=True)
                    m.then_inc(s_sc, 1)
                if real(i + 2):
                    t = i + 2
                    pe.wait_ge(s_xn, t + 1)
                    ge(pe, s_qe, t - 1)
                    for c in range(DC):
                        m = pe.transpose(p_x[:, c * P:(c + 1) * P], xn[:, even, c * P:(c + 1) * P], ident[:])
                    m.then_inc(s_tx, 1)
                if real(i + 1):
                    project_v(i + 1, odd)
                if real(i - 2):
                    t = i - 2
                    pe.wait_ge(s_cl, t + 1)
                    parts(p_o, [([h[:, even, c] for h in hTs], [p[:, WO + c, :] for p in proj]) for c in range(DC)],
                          3).then_inc(s_wo, 1)
                if real(i - 1):
                    t = i - 1
                    pe.wait_ge(s_nm, 2 * (t + 1))
                    if real(i):
                        pe.wait_ge(s_mx, 2 * (i + 1))
                    for g in range(G):
                        for c in range(DC):
                            m = pe.transpose(p_pt[:, g, c * P:(c + 1) * P],
                                             S[:, odd, g, 2 * c:2 * c + 2, :].rearrange("p h k -> p (h k)"), ident[:])
                    m.then_inc(s_pt, 1)
                if real(i + 1):
                    t = i + 1
                    pe.wait_ge(s_qk, t + 1)
                    if real(i + 2):
                        pe.wait_ge(s_xl, t + 2)
                    for n in range(2):
                        for c in range(DC):
                            m = pe.transpose(pT[:, n, c, :], qk[:, n * D + c * P:n * D + (c + 1) * P], ident[:])
                    m.then_inc(s_tq, 1)
                if real(i - 1):
                    t = i - 1
                    pe.wait_ge(s_pe, t + 1)
                    ge(pe, s_res, t)
                    for s in range(2):
                        for c in range(DC):
                            for g in range(G):
                                m = pe.matmul(p_c[32 * g:32 * g + 32, c, 64 * s:64 * s + 64],
                                              vbd[:, (b - 1) % 4, s, G * c + g].rearrange("p h d -> p (h d)"),
                                              PT[:, g, c, 64 * s:64 * s + 64], start=True, stop=True)
                    m.then_inc(s_pv, 1)

            pe.wait_ge(s_id, 2)
            pe.wait_ge(s_tidy, 1)
            over_attention(pe, step)

            def logits(i, b):
                if real(i):
                    pe.wait_ge(s_n2, i + 1)
                    ge(pe, s_e2, i - 3)
                    for c in range(DC):
                        m = pe.transpose(bank[b][:, c * P:(c + 1) * P], x2[:, b, c * P:(c + 1) * P], ident[:])
                    m.then_inc(s_t2, 1)
                if real(i - 2):
                    t = i - 2
                    pe.wait_ge(s_e2, t + 1)
                    for c in range(DC):
                        m = pe.matmul(at_tile(bank[7], t, E), x2T[:, (b - 2) % 4, c, :], gateT[:, c, :], start=(c == 0), stop=(c == DC - 1))
                    m.then_inc(s_lg, 1)

            over_tiles(pe, logits, unroll=4)
            pe.wait_ge(s_oh, 1)
            flat = both.rearrange("p t e -> p (t e)")
            pe.matmul(bank[6][:, 0:NT * E], tri[:], flat, start=True, stop=True)
            pe.matmul(bank[5][:, 0:NT * E], ones[:], flat, start=True, stop=True).then_inc(s_cnt, 1)
            pe.wait_ge(s_pos, 1)
            pe.wait_ge(s_split, NPIECE)
            ffn_pe(pe, "sh", NT)
            ffn_pe(pe, "ex", NE)

        @block.vector
        def _(dve):
            for n in range(4):
                dve.wait_ge(s_x[n], 16)
                for t in range(n * NT // 4, (n + 1) * NT // 4):
                    m = dve.bn_stats(st1[:, t, :], X[:, t, :])
            m.then_inc(s_st, 1)
            dve.wait_ge(s_st, 1)
            for t in range(NT):
                m = dve.bn_aggr(mv1[:, t, :], st1[:, t, :])
            m.then_inc(s_c, 1)
            dve.wait_ge(s_c, 1)
            dve.tensor_scalar(rstd1[:], mv1[:, :, 1], 1e-5, None, ALU.add).then_inc(s_st, 1)
            dve.wait_ge(s_w, N_W)
            cases = [(w_in[:, n, :], csum[:, m, :]) for m, n in enumerate((WQ, WQ + 1, WKM, WKD))]
            cases.append((rows[:, 0:2 * D], bsum[:]))
            for w, s in cases:
                dve.tensor_reduce(s, heads(w), AX.X, ALU.add).then_inc(s_c, 1)
            dve.wait_ge(s_c, 6)
            dve.tensor_scalar(csum[:, 0:4], csum[:, 0:4], 1.0 / HD, None, ALU.mult).then_inc(s_c, 1)
            dve.tensor_scalar(bsum[:], bsum[:], 1.0 / HD, None, ALU.mult).then_inc(s_c, 1)
            dve.wait_ge(s_c, 8)
            for w, s in cases:
                n = s.shape[1]
                dve.tensor_tensor(heads(w), heads(w), s.unsqueeze(2).broadcast_to([w.shape[0], n, HD]), ALU.subtract)
            for par in range(2):
                m = dve.tensor_scalar(kvec[:, par, :], vecs[:, 2:6], par_mask[:, par:par + 1], None, ALU.mult)
            m.then_inc(s_cen, 1)
            dve.wait_ge(s_cen, 1)
            dve.wait_ge(s_wh, 1)
            dve.tensor_tensor(proj[1][:], w_in, proj[0][:].bitcast(F32), ALU.subtract)
            dve.tensor_tensor(rows_r[32:36, :], rows, rows_r[0:4, :].bitcast(F32), ALU.subtract).then_inc(s_tidy, 1)
            dve.wait_ge(s_rt, 1)
            dve.reciprocal(rstd1[:], rstd1[:]).then_inc(s_r1, 1)
            dve.wait_ge(s_r1, 1)
            dve.wait_ge(s_tg, 1)

            def norm_x(t, b):
                ge(dve, s_tx, t - 1)
                dve.tensor_scalar(xn[:, b, :], X[:, t, :], mv1[:, t, 0:1], at_tile(rstd1, t),
                                  ALU.subtract, ALU.mult).then_inc(s_xn, 1)

            def variances(t, b):
                dve.wait_ge(s_sq, t + 1)
                ge(dve, s_rs, t - 1)
                dve.tensor_reduce(var[:, b, :], heads(sq), AX.X, ALU.add).then_inc(s_vr, 1)
                dve.wait_ge(s_vr, t + 1)
                dve.tensor_scalar(var[:, b, :], var[:, b, :], 1.0 / HD, 1e-6, ALU.mult, ALU.add).then_inc(s_seed, 1)
                dve.wait_ge(s_seed, 3 * t + 1)
                dve.tensor_scalar(hv[:, b, :], var[:, b, :], -0.5, None, ALU.mult).then_inc(s_seed, 1)
                dve.tensor_scalar(seed[:, b, :], var[:, b, :].bitcast(I32), 1, None, ALU.arith_shift_right).then_inc(s_seed, 1)
                dve.wait_ge(s_seed, 3 * t + 3)
                dve.tensor_scalar(seed[:, b, :], seed[:, b, :], -1, RSQRT_SEED, ALU.mult, ALU.add).then_inc(s_var, 1)

            def step(i, b):
                even, odd = b % 2, (b + 1) % 2
                if real(i + 1):
                    variances(i + 1, odd)
                if real(i):
                    dve.wait_ge(s_sc, i + 1)
                    ge(dve, s_pt, i - 1)
                    sc = p_sc.rearrange("p g (c k) -> p g c k", k=NK)
                    for n, (k0, k1) in enumerate(((0, NM), (NM, NK))):
                        dve.tensor_reduce(mx[:, even, n], sc[:, :, :, k0:k1], AX.X, ALU.max).then_inc(s_max, 1)
                    dve.wait_ge(s_max, 2 * (i + 1))
                    for n, (k0, k1) in enumerate(((0, NM), (NM, NK))):
                        dve.tensor_tensor(S[:, even, :, :, k0:k1], sc[:, :, :, k0:k1],
                                          mx[:, even, n].unsqueeze(3).broadcast_to([P, G, 4, k1 - k0]),
                                          ALU.subtract).then_inc(s_mx, 1)
                if real(i + 2):
                    t = i + 2
                    dve.wait_ge(s_xh, t + 1)
                    dve.tensor_tensor(xTs[1][:, even].rearrange("p c n -> p (c n)"), p_x,
                                      xTs[0][:, even].rearrange("p c n -> p (c n)").bitcast(F32), ALU.subtract).then_inc(s_xl, 1)
                if real(i - 2):
                    t = i - 2
                    dve.wait_ge(s_wo, t + 1)
                    dve.scalar_tensor_tensor(out=xm[:, even, :], in0=p_o, scalar=tg[:, 0:1], in1=X[:, t, :],
                                             op0=ALU.mult, op1=ALU.add).then_inc(s_res, 1)
                if real(i + 1):
                    t = i + 1
                    dve.wait_ge(s_rs, t + 1)
                    ge(dve, s_tq, t)
                    dve.tensor_tensor(heads(qk), heads(pQK[:]),
                                      ya[:, odd, :].unsqueeze(2).broadcast_to([P, 2 * H, HD]), ALU.mult).then_inc(s_qk, 1)
                if real(i - 2):
                    t = i - 2
                    dve.wait_ge(s_res, t + 1)
                    dve.bn_stats(st2[:, even, :], xm[:, even, :]).then_inc(s_b2, 1)
                    dve.wait_ge(s_b2, 2 * t + 1)
                    dve.tensor_scalar(X[:, t, :], xm[:, even, :], 1.0, None, ALU.mult)
                    dve.bn_aggr(mvr[:, even, :], st2[:, even, :]).then_inc(s_b2, 1)
                    dve.wait_ge(s_b2, 2 * t + 2)
                    dve.tensor_scalar(mv2[:, t, :], mvr[:, even, :], 1.0, None, ALU.mult).then_inc(s_l2, 1)
                if real(i):
                    dve.wait_ge(s_ex, i + 1)
                    ge(dve, s_nm, 2 * (i - 1))
                    for n, (k0, k1) in enumerate(((0, NM), (NM, NK))):
                        dve.tensor_reduce(den[:, even, n, :], S[:, even, :, :, k0:k1].rearrange("p g c k -> p (g c) k"), AX.X,
                                          ALU.add).then_inc(s_sum, 1)
                    dve.wait_ge(s_sum, 2 * (i + 1))
                    dve.reciprocal(den[:, even], den[:, even]).then_inc(s_rd, 1)
                if real(i - 1):
                    t = i - 1
                    dve.wait_ge(s_ch, t + 1)
                    dve.tensor_tensor(hTs[1][:, odd, 0:DC], p_c, hTs[0][:, odd, 0:DC].bitcast(F32),
                                      ALU.subtract).then_inc(s_cl, 1)
                if real(i + 3):
                    norm_x(i + 3, odd)

            norm_x(0, 0)
            over_attention(dve, step)

            dve.wait_ge(s_l2, NT)
            dve.tensor_scalar(rstd2[:], mv2[:, :, 1], 1e-5, None, ALU.add).then_inc(s_v2, 1)
            dve.wait_ge(s_rt2, 1)
            dve.reciprocal(rstd2[:], rstd2[:]).then_inc(s_r2, 1)
            dve.wait_ge(s_r2, 1)

            def norm_2(i, b):
                return dve.tensor_scalar(x2[:, b, :], X[:, i, :], mv2[:, i, 0:1],
                                         rstd2[:, i:i + 1] if isinstance(i, int) else rstd2[:, bass.ds(i, 1)],
                                         ALU.subtract, ALU.mult)

            def x2_step(i, b):
                if real(i):
                    ge(dve, s_t2, i - 3)
                    norm_2(i, b).then_inc(s_n2, 1)

            over_tiles(dve, x2_step, unroll=4)
            route(dve)

            def x2_again(i, b):
                ge(dve, ffn["sh"]["xt"], i - 3)
                ge(dve, s_sc1[b], passes(i, b, 32))
                norm_2(i, b).then_inc(ffn["sh"]["x"], 1)

            ffn_dve(dve, "sh", NT, x2_again)
            ffn_dve(dve, "ex", NE, None)
            dve.tensor_scalar(w1, w1, tg[:, 1:2], None, ALU.mult).then_inc(s_o1, 1)
            dve.tensor_scalar(w2, w2, tg[:, 1:2], None, ALU.mult).then_inc(s_o1, 1)
            dve.wait_ge(s_o1, 2)

            def combine(i, b):
                if real(i):
                    dve.wait_ge(s_g[b], passes(i, b, 32) + 32)
                    wa, wb = (w[:, i:i + 1] if isinstance(i, int) else w[:, bass.ds(i, 1)] for w in (w1, w2))
                    dve.scalar_tensor_tensor(out=g1[:, b, :], in0=g1[:, b, :], scalar=wa, in1=X[:, i, :],
                                             op0=ALU.mult, op1=ALU.add).then_inc(s_o1, 1)
                    dve.wait_ge(s_o1, i + 3)
                    dve.scalar_tensor_tensor(out=g2[:, b, :], in0=g2[:, b, :], scalar=wb, in1=g1[:, b, :],
                                             op0=ALU.mult, op1=ALU.add).then_inc(s_cmb, 1)

            over_tiles(dve, combine, unroll=4)


def layout(np, i):
    f = lambda n: np.asarray(i[n])
    T, D = 4096, 256
    HD = 16
    wkv = np.concatenate([f("L0_xattn_Wk"), f("L0_xattn_Wv")], axis=1).reshape(128, 16, 2, HD)
    bkv = np.concatenate([f("L0_xattn_bk"), f("L0_xattn_bv")]).reshape(16, 2, HD)
    wd = f("L0_xattn_Wkv_dca").reshape(128, 2, 16, HD)
    bd = f("L0_xattn_bkv_dca").reshape(2, 16, HD)
    flat = lambda w: np.ascontiguousarray(w.reshape(w.shape[0], -1))
    rows = np.zeros((4, 4, D), np.float32)
    rows[0, 0] = f("L0_xattn_bq")
    rows[1, 1], rows[2, 1] = bkv[:, 0].ravel(), bd[0].ravel()
    rows[1, 2], rows[2, 2] = bkv[:, 1].ravel(), bd[1].ravel()
    rows[0, 3] = f("L0_xattn_bo")
    masks = np.zeros((64, 2, 64), np.float32)
    for r in (0, 32):
        masks[r] = 1
        masks[r + 1, :, :48] = 1
        masks[r + 2, :, 48:] = 1
    vec = [np.tile(f("L0_xattn_" + n), 8) for n in ("qn_w", "qn_b", "kn_w", "kn_b", "kn_dca_w", "kn_dca_b")]
    par = (np.arange(128) // HD % 2)
    def lay(w):
        k = w.shape[0]
        w = np.concatenate([w, np.zeros((-k % 128,) + w.shape[1:], w.dtype)])
        return np.ascontiguousarray(w.reshape(-1, 128, *w.shape[1:]).swapaxes(0, 1)).reshape(128, -1)
    w_all = np.concatenate([
        lay(np.concatenate([f("L0_ffn_w_gate"), f("L0_ffn_w_up")], axis=1).transpose(2, 0, 1)),
        lay(f("L0_ffn_w_down").transpose(2, 0, 1)),
        lay(np.concatenate([f("L0_ffn_sw_gate"), f("L0_ffn_sw_up")], axis=0).T),
        lay(f("L0_ffn_sw_down").T)], axis=1)
    return {
        "x": f("x").reshape(T, D), "ctxT": np.ascontiguousarray(f("ctx_1024").reshape(T, 128).T),
        "wq": f("L0_xattn_Wq"), "wkv": np.stack([flat(w) for w in (wkv[:, :, 0], wkv[:, :, 1], wd[:, 0], wd[:, 1])]),
        "wo": f("L0_xattn_Wo"),
        "rows": rows.reshape(4, 4 * D), "row_masks": masks.reshape(64, 128),
        "vecs": np.stack(vec, axis=1), "par_mask": np.stack([1 - par, par], 1).astype(np.float32),
        "g_xattn": f("g_xattn"), "g_ffn": f("g_ffn"),
        "gateT": np.ascontiguousarray(f("L0_ffn_gate_weight").T),
        "w_all": w_all,
        "tri": np.triu(np.ones((128, 128), np.float32), 1), "ones": np.ones((128, 128), np.float32),
        "e_idx": np.tile(np.arange(8, dtype=np.float32), (128, 1)),
        "j_idx": np.tile(np.arange(72, dtype=np.float32), (128, 1)),
    }


def kernel(**inputs):
    import numpy as _np
    import concourse.bacc as _bacc
    from concourse.bass_utils import run_bass_kernel_spmd as _run

    nc = _bacc.Bacc("TRN2", target_bir_lowering=False, num_devices=1)
    arrays, aps = {}, {}
    for name, array in layout(_np, inputs).items():
        array = _np.ascontiguousarray(array)
        arrays[f"in_{name}_dram"] = array
        aps[name] = nc.dram_tensor(f"in_{name}_dram", array.shape, mybir.dt.from_np(array.dtype), kind="ExternalInput").ap()
    out = nc.dram_tensor("out_dram", (4096, 256), F32, kind="ExternalOutput").ap()
    gated_cross_attention_and_moe(nc, aps, out)
    r = _run(nc, [arrays], core_ids=[0])
    return r.results[0]["out_dram"].reshape(64, 64, 256)
```

```python
from contextlib import ExitStack

import concourse.bass as bass
from concourse import mybir

ALU = mybir.AluOpType
ACT = mybir.ActivationFunctionType
AX = mybir.AxisListType
F32 = mybir.dt.float32
F32R = mybir.dt.float32r
I32 = mybir.dt.int32
P = 128


def gated_cross_attention_and_moe(nc, a, out):
    T, D = a["x"].shape
    W = D + 2
    NS = 64
    NM, ND = 48, 16
    NK = NM + ND
    HD = 16
    H = D // HD
    NT = T // P
    DC = D // P
    G = P // 32
    LATE = 8
    NX = 8
    EARLY = 4
    UNPLACED = 7
    NG = 8
    SCALE = float(HD) ** -0.5
    RSQRT_SEED = 0x5F3759DF
    E = a["gateT"].shape[1]
    EBITS = (E - 1).bit_length()
    F = 176
    FS = 2 * F
    NE = (2 * T + E * (P - 1)) // P
    NE += -NE % 8
    CUTS = {k: [(c, min(c + P, n)) for c in range(0, n, P)] for k, n in (("sh", FS), ("ex", F), ("late", FS))}

    with ExitStack() as ctx:
        def sb(name, shape, dt=F32):
            return ctx.enter_context(nc.sbuf_tensor(name, shape, dt))

        def pb(name, shape, dt=F32):
            return ctx.enter_context(nc.psum_tensor(name, shape, dt))

        def sem(name):
            return ctx.enter_context(nc.semaphore(name))

        ident = sb("ident", [P, P])
        proj = [sb(f"proj_{n}", [P, 8, D], F32R) for n in "hl"]
        WQ, WKM, WVM, WKD, WVD, WO = 0, 2, 3, 4, 5, 6
        rows_r = sb("rows_r", [64, 4 * D], F32R)
        masks_r = sb("masks_r", [64, P], F32R)
        vecs = sb("vecs", [P, 6])
        gates = sb("gates", [P, 2])
        tg = sb("tg", [P, 2])
        par_mask = sb("par_mask", [P, 2])
        kvec = sb("kvec", [P, 2, 4])
        csum = sb("csum", [P, 5, H])
        bsum = sb("bsum", [4, 2 * H])
        gateT = sb("gateT", [P, DC, E])
        e_idx = sb("e_idx", [P, E])
        tok_idx = sb("tok_idx", [P, NT])
        WALL = a["w_all"].shape[1]
        PIECE = 384
        NPIECE = WALL // PIECE
        w_all = [sb(f"w_all_{n}", [P, WALL], F32R) for n in "hl"]
        at = 0
        views = []
        for chunks, width in ((DC, E * 2 * F), (2, E * D), (DC, 2 * FS), (3, D)):
            views.append([w[:, at:at + chunks * width].rearrange("p (c n) -> p c n", c=chunks) for w in w_all])
            at += chunks * width
        gu, dn, sgu, sdn = views
        assert at == WALL and WALL % PIECE == 0 and NPIECE <= NT
        yTs = [sb(f"yT_{n}", [P, 2, 2, 2, NK], F32R) for n in "hl"]
        xTs = [sb(f"xT_{n}", [P, 2, DC, P], F32R) for n in "hl"]
        hTs = [sb(f"hT_{n}", [P, 2, 3, P], F32R) for n in "hl"]
        idx = sb("idx", [P, NX, 2], mybir.dt.uint32)
        late_idx = sb("late_idx", [P, LATE, 2], mybir.dt.uint32)
        dest = sb("dest", [P, 4, 1], mybir.dt.uint32)
        c15 = sb("c15", [P, 2 * H + 1])
        pad_row = sb("pad_row", [P, W])
        X = sb("X", [P, NT, D])
        st1 = sb("st1", [P, NT, 6])
        mv1 = sb("mv1", [P, NT, 2])
        rstd1 = sb("rstd1", [P, NT])
        rstd2 = sb("rstd2", [P, NT])
        st2 = sb("st2", [P, 2, 6])
        mvr = sb("mvr", [P, 2, 2])
        mv2 = sb("mv2", [P, NT, 2])
        ARENA = 10 * 1024 + 992
        arena = sb("arena", [P, ARENA])
        used = [0]

        def take(*shape, dt=F32):
            n = 1
            for d in shape:
                n *= d
            at, used[0] = used[0], used[0] + n
            assert used[0] <= ARENA
            ap = arena[:, at:at + n]
            if dt != F32:
                ap = ap.bitcast(dt)
            names = "abcde"[:len(shape)]
            return ap.rearrange("p (" + " ".join(names) + ") -> p " + " ".join(names),
                                **dict(zip(names, shape))) if len(shape) > 1 else ap

        y_in = take(2, P)
        stage = take(2, PIECE)
        xn = take(2, D)
        sq = take(2 * D)
        NV = 2 * H + 1
        var = take(2, NV)
        hv = take(2, NV)
        seed = take(2, NV, dt=I32)
        ya = take(2, NV)
        yt = take(2, NV)
        qk = take(2, 2 * D)
        qT = take(2, DC, P)
        kT = take(2, DC * 2, 2, NK).rearrange("p b (c h) s k -> p b c h s k", c=DC)
        vbd = take(4, 2, H // 2, 2 * HD).rearrange("p b s j (h d) -> p b s j h d", h=2)
        S = take(2, G, 4, NK)
        w_in = S.rearrange("p b g c k -> p (b g c k)").rearrange("p (c n) -> p c n", c=8)
        mx = take(2, 2, G, 4)
        den = take(2, 2, H)
        PT = take(G, DC, P)
        early = PT.rearrange("p g c n -> p (g c n)")
        xm = take(2, D)
        rows = early[0:4, 0:4 * D]
        row_masks = xm.rearrange("p b d -> p (b d)")[0:64, 0:P]
        x2a = take(D)
        x2aT = take(DC, P)

        used[0] = 0
        sg = take(2, FS)
        hid = take(2, FS)
        late_row = take(LATE, W)
        g = arena[:, used[0]:used[0] + NG * 2 * D].rearrange("p (b r d) -> p b r d", b=NG, r=2)
        g_end = used[0] + NG * 2 * D
        x2_row = take(NX, W)
        x2 = x2_row[:, :, 0:D]
        rows_in = take(4, W)
        y_sb = take(4, D)
        assert used[0] >= g_end
        rank_off = take(4)
        pad_off = take(4)
        token_e1 = take(NT, 2)
        tri = take(P)
        ones = take(P)
        j_idx = take(NE)
        place_value = take(NE)
        lg = take(NT, E)
        oh1 = take(NT, E)
        oh2 = take(NT, E)
        both = take(NT, E)
        pfx = take(NT, E)
        cumA = take(NT, E)
        cumB = take(NT, E)
        cand = take(NT, E)
        r1 = take(NT)
        r2 = take(NT)
        w1 = take(NT)
        w2 = take(NT)
        wsum = take(NT)
        pos = take(NT, 2)
        tiles_f = take(E)
        tiles_i = take(E, dt=I32)
        endA = take(E)
        endB = take(E)
        start = take(E)
        ge_end = take(NE, E)
        te_f = take(NE)
        te8 = take(NE // 8)
        te = take(NE // 8, dt=I32)

        pS = pb("pS", [P, G, 512])
        p_sc = pS[:, :, 0:256]
        p_pt = pS[:, :, 256:512]
        pQK = pb("pQK", [P, 512])
        pV = pb("pV", [P, 512])
        p_v = pV[:, 0:D]
        p_logits = pV[:, 256:256 + NT * E]
        pT = pb("pT", [P, 2, DC, P])
        p_x = pT[:, 0].rearrange("p c n -> p (c n)")
        pCO = pb("pCO", [P, 512])
        p_c = pCO[:, 0:256].rearrange("p (c n) -> p c n", c=DC)
        p_o = pCO[:, 256:512]

        s_w, s_k = sem("weights_loaded"), sem("constants_loaded")
        s_x = [sem(f"x_loaded{n}") for n in range(4)]
        s_id = sem("identity_made")
        s_ws = [sem(f"staged{n}") for n in range(2)]
        s_high, s_split = sem("weights_high"), sem("weights_split")
        s_yz, s_yh = sem("y_zeros"), sem("y_high")
        s_wh, s_rh = sem("proj_high"), sem("biases_high")
        s_tidy = sem("proj_ready")
        s_zf = sem("rows_zeroed")
        s_tri = sem("router_constants_loaded")
        s_v1, s_v2 = sem("variances_set"), sem("ln2_var")
        s_n2, s_t2, s_e2, s_lg = sem("x2_ready"), sem("x2T_in_psum"), sem("x2T_ready"), sem("logits_ready")
        s_rx, s_rs_, s_oh, s_cnt = sem("router_exp_in"), sem("router_step"), sem("choices_ready"), sem("counts_ready")
        s_re, s_pos, s_te = sem("router_exp"), sem("positions_ready"), sem("tile_experts_ready")
        s_sc1 = [sem(f"rows_scattered{n}") for n in range(NX)]
        s_xs = [sem(f"expert_rows_loaded{n}") for n in range(4)]
        s_ys = [sem(f"expert_outputs_scattered{n}") for n in range(4)]
        s_g = [sem(f"outputs_loaded{n}") for n in range(NG)]
        s_late = sem("late_rows_scattered")
        s_second, s_dest = sem("rank_known"), sem("destination_ready")
        s_cmb, s_o1 = sem("combined"), sem("first_added")
        s_os = [sem(f"tile_stored{n}") for n in range(NG)]
        ffn = {k: {n: sem(f"{k}_{n}") for n in
                   ("x", "xt", "xh", "xl", "gu", "silu", "h", "ht", "hh", "hl", "y", "yd")} for k in ("sh", "ex", "late")}
        s_yl = [sem(f"y_loaded{n}") for n in range(2)]
        s_y = sem("y_spread")
        s_cen = sem("weights_centred")
        s_c = sem("centring_step")
        s_zero = sem("zeros_written")
        s_bn, s_mv, s_st = sem("ln1_bn"), sem("ln1_means"), sem("ln1_stats")
        s_rt = sem("ln1_roots")
        s_r1 = sem("ln1_rstd")
        s_tg = sem("gates_ready")
        s_xn, s_tx, s_xh, s_xl = sem("xn_ready"), sem("xnT_in_psum"), sem("xnT_high"), sem("xnT_rest")
        s_pqk, s_raw, s_proj = sem("qk_projected"), sem("qk_copied"), sem("v_projected")
        s_sq, s_vev = sem("squared"), sem("v_ready")
        s_vr, s_seed, s_var = sem("var_summed"), sem("seed_shifted"), sem("seed_ready")
        s_nw, s_rs = sem("newton_step"), sem("rstd_ready")
        s_qk, s_tq, s_qe = sem("qk_normed"), sem("qkT_in_psum"), sem("qkT_ready")
        s_sc, s_max, s_mx = sem("scores_ready"), sem("max_ready"), sem("max_subtracted")
        s_ex, s_sum, s_rd = sem("exp_ready"), sem("sums_ready"), sem("reciprocal_ready")
        s_nm, s_pt, s_pe = sem("probs_ready"), sem("probsT_in_psum"), sem("probsT_ready")
        s_pv, s_ch, s_cl, s_wo = sem("ctxT_in_psum"), sem("ctxT_high"), sem("ctxT_rest"), sem("attn_out")
        s_res, s_b2, s_mvr, s_l2 = sem("residual_added"), sem("ln2_bn"), sem("ln2_aggregated"), sem("ln2_stats")
        s_xw = [sem(f"x_replaced{n}") for n in range(2)]

        s_passed = {nc.gpsimd: sem("pool_passed"), nc.tensor: sem("pe_passed"), nc.scalar: sem("act_passed")}

        block = ctx.enter_context(nc.Block())

        def ge(eng, s, value):
            if not isinstance(value, int) or value > 0:
                eng.wait_ge(s, value)

        def settle(eng):
            eng.sem_inc(s_passed[eng], 1)

        def over_tiles(eng, step, n=NT, unroll=2, low=0, ahead=2, behind=1):
            first = max(unroll, -(-behind // unroll) * unroll)
            rounds = max(0, (n - ahead - first) // unroll)
            for i in range(low, min(first, n + max(behind, 2))):
                step(i, i % unroll)
            if rounds:
                with eng.Fori(first // unroll, first // unroll + rounds) as r:
                    for b in range(unroll):
                        step(r * unroll + b, b)
            for i in range(first + rounds * unroll, n + max(behind, 2)):
                step(i, i % unroll)

        def over_attention(eng, step):
            over_tiles(eng, step, NT, 4, -3, 4, behind=5)

        def passes(t, b, each, ring=4):
            return (t // ring) * each if isinstance(t, int) else (t - b) * (each // ring)

        def at_tile(ap, t, width=1):
            return ap[:, t * width:(t + 1) * width] if isinstance(t, int) else ap[:, bass.ds(t * width, width)]

        def real(t, n=NT):
            return not isinstance(t, int) or 0 <= t < n

        def heads(ap):
            return ap.rearrange("p (h d) -> p h d", d=HD)

        xs = nc.dram_tensor("rows_by_expert", [NE * P, W], F32, kind="Internal").ap()
        ys = nc.dram_tensor("outputs_by_token", [2 * T + 4 * P, D], F32, kind="Internal").ap()

        def row_tile(dram, t):
            return dram[t * P:(t + 1) * P] if isinstance(t, int) else dram[bass.ts(t, P)]

        bank = [pS[:, 0, :], pS[:, 1, :], pS[:, 2, :], pS[:, 3, :], pQK[:], pV[:],
                pT[:].rearrange("p a c n -> p (a c n)"), pCO[:]]

        def gate_up(k, b):
            if k != "ex":
                return bank[2 * b][:, 0:FS], bank[2 * b + 1][:, 0:FS]
            return bank[2 * b][:, 0:F], bank[2 * b][:, F:2 * F]

        p_xT, p_hT, p_y = bank[4], bank[5], bank[6]

        def with_more(step, after):
            def more(i, b):
                step(i, b)
                for f in after.get(i, ()) if isinstance(i, int) else ():
                    f()
            return more


        def ffn_pe(pe, k, n, after={}):
            U = 8
            s, cuts = ffn[k], CUTS[k]
            if k == "ex":
                eight = pe.alloc_register("experts_of_eight")
                regs = [pe.alloc_register(f"expert{m}") for m in range(4)]
                pe.wait_ge(s_te, 1)
                settle(pe)

            def load_expert(t, tb):
                if tb == 0:
                    r = t // 8
                    pe.reg_load(eight, te[0:1, r:r + 1] if isinstance(t, int) else te[0:1, bass.ds(r, 1)])
                pe.reg_alu(regs[tb % 4], eight, EBITS * tb, ALU.logical_shift_right)
                pe.reg_alu(regs[tb % 4], regs[tb % 4], (1 << EBITS) - 1, ALU.bitwise_and)

            def products(dst, pairs):
                last = len(pairs) - 1
                for m, ((xh, xl), (wh, wl)) in enumerate(pairs):
                    pe.matmul(dst, xh, wl, start=(m == 0), stop=False)
                    pe.matmul(dst, xl, wh, start=False, stop=False)
                    r = pe.matmul(dst, xh, wh, start=False, stop=(m == last))
                return r

            def step(i, b):
                b2, o = b % 2, 1 - b % 2

                def transpose_x(t, tb):
                    if k != "ex":
                        pe.wait_ge(s["x"], t + 1)
                        src = x2[:, tb, :] if k == "sh" else late_row[:, tb, 0:D]
                    else:
                        r = tb % 4
                        pe.wait_ge(s_xs[r], passes(t, r, 16) + 16)
                        src = rows_in[:, r, :]
                    ge(pe, s["xl"], t)
                    for c in range(DC):
                        m = pe.transpose(p_xT[:, c * P:(c + 1) * P], src[:, c * P:(c + 1) * P], ident[:])
                    m.then_inc(s["xt"], 1)

                if isinstance(i, int) and i == 0:
                    transpose_x(0, 0)
                    if k == "ex":
                        load_expert(0, 0)
                if real(i + 1, n):
                    transpose_x(i + 1, (b + 1) % U)
                if real(i - 1, n):
                    pe.wait_ge(s["h"], i)
                    ge(pe, s["hl"], i - 1)
                    for m, (k0, k1) in enumerate(cuts):
                        r = pe.transpose(p_hT[0:k1 - k0, m * P:(m + 1) * P], hid[:, o, k0:k1], ident[:])
                    r.then_inc(s["ht"], 1)
                if real(i, n):
                    pe.wait_ge(s["xl"], i + 1)
                    ge(pe, s["h"], i - 1)
                    x = [(xTs[0][:, b2, c, :], xTs[1][:, b2, c, :]) for c in range(DC)]
                    if k != "ex":
                        for m, dst in enumerate(gate_up(k, b2)):
                            r = products(dst, [(x[c], [w[:, c, m * FS:(m + 1) * FS] for w in sgu]) for c in range(DC)])
                    else:
                        e = pe.snap(regs[b % 4], min_val=0, max_val=E - 1)
                        cols = bass.ds(e * (2 * F), 2 * F)
                        r = products(bank[2 * b2][:, 0:2 * F], [(x[c], [w[:, c, cols] for w in gu]) for c in range(DC)])
                    r.then_inc(s["gu"], 1)
                if k == "ex" and real(i + 1, n):
                    load_expert(i + 1, (b + 1) % 8)
                if real(i - 2, n):
                    t = i - 2
                    pe.wait_ge(s["hl"], t + 1)
                    ge(pe, s["yd"], t)
                    h = [(hTs[0][0:k1 - k0, b2, m, :], hTs[1][0:k1 - k0, b2, m, :]) for m, (k0, k1) in enumerate(cuts)]
                    if k != "ex":
                        w = [[w[0:k1 - k0, m, :] for w in sdn] for m, (k0, k1) in enumerate(cuts)]
                    else:
                        e = pe.snap(regs[(b - 2) % 4], min_val=0, max_val=E - 1)
                        w = [[w[0:k1 - k0, m, bass.ds(e * D, D)] for w in dn] for m, (k0, k1) in enumerate(cuts)]
                    products(p_y[:, 0:D], list(zip(h, w))).then_inc(s["y"], 1)

            over_tiles(pe, with_more(step, after), n, U)

        def ffn_act(act, k, n):
            s, cuts = ffn[k], CUTS[k]

            def high_x(t, b):
                act.wait_ge(s["xt"], t + 1)
                ge(act, s["gu"], t - 1)
                act.activation(xTs[0][:, b].rearrange("p c n -> p (c n)"), p_xT[:, 0:D], ACT.Copy).then_inc(s["xh"], 1)

            def step(i, b):
                e, o = b % 2, 1 - b % 2
                if isinstance(i, int) and i == 0:
                    high_x(0, 0)
                if real(i + 1, n):
                    high_x(i + 1, o)
                if real(i - 1, n):
                    act.wait_ge(s["ht"], i)
                    ge(act, s["y"], i - 2)
                    for m, (k0, k1) in enumerate(cuts):
                        r = act.activation(hTs[0][0:k1 - k0, o, m, :], p_hT[0:k1 - k0, m * P:(m + 1) * P], ACT.Copy)
                    r.then_inc(s["hh"], 1)
                if real(i, n):
                    act.wait_ge(s["gu"], i + 1)
                    ge(act, s["h"], i - 1)
                    act.activation(sg[:, e, 0:cuts[-1][1]], gate_up(k, e)[0], ACT.Silu).then_inc(s["silu"], 1)
                if k == "ex" and real(i - 2, n):
                    act.wait_ge(s["y"], i - 1)
                    r = (b - 2) % 4
                    ge(act, s_ys[r], passes(i - 2, r, 16))
                    act.activation(y_sb[:, r, :], p_y[:, 0:D], ACT.Copy).then_inc(s["yd"], 1)

            over_tiles(act, step, n, 4)

        def ffn_dve(dve, k, n, make_x, after={}):
            U = NX if k == "sh" else 4
            s, cuts = ffn[k], CUTS[k]

            def rest_x(t, b):
                dve.wait_ge(s["xh"], t + 1)
                ge(dve, s["gu"], t - 1)
                dve.tensor_tensor(xTs[1][:, b].rearrange("p c n -> p (c n)"), p_xT[:, 0:D],
                                  xTs[0][:, b].rearrange("p c n -> p (c n)").bitcast(F32), ALU.subtract).then_inc(s["xl"], 1)

            def step(i, b):
                e, o = b % 2, 1 - b % 2
                if isinstance(i, int) and i == 0:
                    if make_x:
                        for t in range(3):
                            make_x(t, t)
                    rest_x(0, 0)
                if real(i + 1, n):
                    rest_x(i + 1, o)
                if real(i - 1, n):
                    dve.wait_ge(s["hh"], i)
                    ge(dve, s["y"], i - 2)
                    for m, (k0, k1) in enumerate(cuts):
                        r = dve.tensor_tensor(hTs[1][0:k1 - k0, o, m, :], p_hT[0:k1 - k0, m * P:(m + 1) * P],
                                              hTs[0][0:k1 - k0, o, m, :].bitcast(F32), ALU.subtract)
                    r.then_inc(s["hl"], 1)
                if real(i, n):
                    dve.wait_ge(s["silu"], i + 1)
                    ge(dve, s["ht"], i - 1)
                    w = cuts[-1][1]
                    dve.tensor_tensor(hid[:, e, 0:w], sg[:, e, 0:w], gate_up(k, e)[1], ALU.mult).then_inc(s["h"], 1)
                if make_x and real(i + 3, n):
                    make_x(i + 3, (b + 3) % U)
                if k == "ex" and real(i, n):
                    dve.wait_ge(s_xs[b], passes(i, b, 16) + 16)
                    dve.tensor_scalar(rank_off[:, b:b + 1], rows_in[:, b, D + 1:W], at_tile(te_f, i), 1.0,
                                      ALU.not_equal, ALU.mult).then_inc(s_second, 1)
                    dve.tensor_scalar(pad_off[:, b:b + 1], rows_in[:, b, D + 1:W], -1.0, float(P * b),
                                      ALU.is_equal, ALU.mult).then_inc(s_second, 1)
                    dve.wait_ge(s_second, 2 * i + 2)
                    ge(dve, s_ys[b], passes(i, b, 16))
                    dve.scalar_tensor_tensor(out=dest[:, b, :], in0=rank_off[:, b:b + 1], scalar=rows_in[:, b, D:D + 1],
                                             in1=pad_off[:, b:b + 1], op0=ALU.add, op1=ALU.add).then_inc(s_dest, 1)
                if k != "ex" and real(i - 2, n):
                    t = i - 2 if k == "sh" else i - 2 + NT - LATE
                    dve.wait_ge(s["y"], i - 1)
                    dve.scalar_tensor_tensor(out=X[:, t, :], in0=p_y[:, 0:D], scalar=tg[:, 1:2], in1=X[:, t, :],
                                             op0=ALU.mult, op1=ALU.add).then_inc(s["yd"], 1)

            over_tiles(dve, with_more(step, after), n, U, ahead=3)

        def router(dve):
            count = [0]
            p_counts = bank[7].rearrange("p (n t e) -> p n t e", n=2, e=E)
            sums = {}

            def done(ins):
                count[0] += 1
                ins.then_inc(s_rs_, 1)
                dve.wait_ge(s_rs_, count[0])

            def over_e(v):
                return v.unsqueeze(2).broadcast_to([P, NT, E])

            def over_t(v):
                return v.unsqueeze(1).broadcast_to([P, NT, E])

            def exponents():
                dve.wait_ge(s_lg, NT)
                dve.tensor_copy(token_e1[:, :, 0], tok_idx[:])
                p_lg = p_logits.rearrange("p (t e) -> p t e", e=E)
                done(dve.tensor_reduce(r1, p_lg, AX.X, ALU.max))
                dve.tensor_tensor(lg, p_lg, over_e(r1), ALU.subtract).then_inc(s_rx, 1)

            def choose():
                dve.wait_ge(s_re, 1)
                done(dve.tensor_reduce(r1, lg, AX.X, ALU.add))
                done(dve.reciprocal(r1, r1))
                done(dve.tensor_tensor(lg, lg, over_e(r1), ALU.mult))
                e1 = token_e1[:, :, 1]
                for w, oh, e in ((w1, oh1, e1), (w2, oh2, r2)):
                    done(dve.tensor_reduce(w, lg, AX.X, ALU.max))
                    done(dve.tensor_tensor(cand, lg, over_e(w), ALU.is_lt))
                    done(dve.scalar_tensor_tensor(out=cand, in0=cand, scalar=float(E), in1=over_t(e_idx[:]),
                                                  op0=ALU.mult, op1=ALU.add))
                    done(dve.tensor_reduce(e, cand, AX.X, ALU.min))
                    done(dve.tensor_tensor(oh, over_t(e_idx[:]), over_e(e), ALU.is_equal))
                    if w is w1:
                        done(dve.scalar_tensor_tensor(out=lg, in0=oh, scalar=-2.0, in1=lg, op0=ALU.mult, op1=ALU.add))
                dve.tensor_tensor(both, oh1, oh2, ALU.add).then_inc(s_oh, 1)
                dve.tensor_scalar(x2_row[:, 0:EARLY, D:W], token_e1[:, 0:EARLY, :], 1.0, None, ALU.mult)

            def weights():
                done(dve.tensor_tensor(wsum, w1, w2, ALU.add))
                done(dve.tensor_scalar(wsum, wsum, 1e-20, None, ALU.add))
                done(dve.reciprocal(wsum, wsum))
                done(dve.tensor_tensor(w1, w1, wsum, ALU.mult))
                done(dve.tensor_tensor(w2, w2, wsum, ALU.mult))

            def prefix():
                dve.wait_ge(s_cnt, 1)
                done(dve.tensor_copy(cumA, p_counts[:, 1]))
                src, dst, d = cumA, cumB, 1
                while d < NT:
                    done(dve.tensor_copy(dst[:, 0:d, :], src[:, 0:d, :]))
                    done(dve.tensor_tensor(dst[:, d:NT, :], src[:, d:NT, :], src[:, 0:NT - d, :], ALU.add))
                    src, dst, d = dst, src, 2 * d
                done(dve.tensor_tensor(pfx, src, p_counts[:, 0], ALU.add))
                done(dve.tensor_tensor(pfx, pfx, p_counts[:, 1], ALU.subtract))
                sums["tiles"] = src

            def starts():
                src = sums["tiles"]
                done(dve.tensor_scalar(tiles_f, src[:, NT - 1, :], float(P - 1), None, ALU.add))
                done(dve.tensor_copy(tiles_i, tiles_f))
                done(dve.tensor_scalar(tiles_i, tiles_i, 7, None, ALU.arith_shift_right))
                done(dve.tensor_copy(tiles_f, tiles_i))
                done(dve.tensor_copy(endA, tiles_f))
                a_, b_, d = endA, endB, 1
                while d < E:
                    done(dve.tensor_copy(b_[:, 0:d], a_[:, 0:d]))
                    done(dve.tensor_tensor(b_[:, d:E], a_[:, d:E], a_[:, 0:E - d], ALU.add))
                    a_, b_, d = b_, a_, 2 * d
                done(dve.tensor_tensor(start, a_, tiles_f, ALU.subtract))
                done(dve.tensor_scalar(start, start, float(P), None, ALU.mult))
                done(dve.tensor_tensor(pfx, pfx, over_t(start), ALU.add))
                sums["ends"] = a_

            def positions():
                for n, oh in enumerate((oh1, oh2)):
                    done(dve.tensor_tensor(cand, oh, pfx, ALU.mult))
                    done(dve.tensor_reduce(pos[:, :, n], cand, AX.X, ALU.add))
                dve.tensor_copy(idx[:, 0:UNPLACED, :], pos[:, 0:UNPLACED, :]).then_inc(s_pos, 1)

            def tile_experts():
                dve.wait_ge(s_tri, 4 * 16)
                a_ = sums["ends"]
                done(dve.tensor_tensor(ge_end, j_idx.unsqueeze(2).broadcast_to([P, NE, E]),
                                       a_.unsqueeze(1).broadcast_to([P, NE, E]), ALU.is_ge))
                done(dve.tensor_reduce(te_f, ge_end, AX.X, ALU.add))
                done(dve.tensor_scalar(te_f, te_f, float(E - 1), None, ALU.min))
                done(dve.tensor_tensor(ge_end[:, :, 0], te_f, place_value, ALU.mult))
                done(dve.tensor_reduce(te8, ge_end[:, :, 0].rearrange("p (r m) -> p r m", m=8), AX.X, ALU.add))
                dve.tensor_copy(te, te8).then_inc(s_te, 1)

            return exponents, choose, prefix, starts, positions, weights, tile_experts

        N_W, N_K = 9 * 16, 4 * 16
        Q = NT // 4
        LATE_AFTER = (1, 3, 5, 7, 16, 18, 20, 22)
        ZERO, ZERO_FROM = 3, 4

        @block.sync
        def _(sp):
            def load_y(t, b):
                if real(t):
                    ge(sp, s_y, t - 1)
                    src = a["ctxT"][:, bass.ts(t, P)] if not isinstance(t, int) else a["ctxT"][:, t * P:(t + 1) * P]
                    sp.dma_start(y_in[:, b, :], src).then_inc(s_yl[b], 16)

            for dst, src in (
                (w_in[:, WQ:WQ + DC], a["wq"].rearrange("(c p) n -> p c n", p=P)),
                (w_in[:, WKM:WKM + 4], a["wkv"].rearrange("w p n -> p w n")),
                (rows, a["rows"]), (vecs[:], a["vecs"]), (par_mask[:], a["par_mask"]), (row_masks, a["row_masks"]),
                (w_in[:, WO:WO + DC], a["wo"].rearrange("(c p) n -> p c n", p=P)),
                (gates[:, 0:1], a["g_xattn"].rearrange("(a n) -> a n", a=1).partition_broadcast(P)),
                (gates[:, 1:2], a["g_ffn"].rearrange("(a n) -> a n", a=1).partition_broadcast(P)),
            ):
                sp.dma_start(dst, src).then_inc(s_w, 16)
            for n in range(4):
                sp.dma_start(X[:, n * Q:(n + 1) * Q, :],
                             a["x"].rearrange("(t p) d -> p t d", p=P)[:, n * Q:(n + 1) * Q, :]).then_inc(s_x[n], 16)
                if n == 0:
                    load_y(0, 0)
            for dst, src in (
                (gateT[:], a["gateT"].rearrange("(c p) n -> p c n", p=P)),
                (pad_row[:, D:W], a["pad"]), (e_idx[:], a["e_idx"]), (tok_idx[:], a["tok_idx"]),
            ):
                sp.dma_start(dst, src).then_inc(s_k, 16)

            def attention_io(i, b):
                load_y(i + 4, b % 2)
                if real(i, NPIECE):
                    ge(sp, s_split, i - 1)
                    sp.dma_start(stage[:, b % 2, :], at_tile(a["w_all"], i, PIECE)).then_inc(s_ws[b % 2], 16)
                if real(i - 2):
                    t = i - 2
                    sp.wait_ge(s_res, t + 1)
                    sp.dma_start(X[:, t, :] if isinstance(t, int) else X[:, bass.ds(t, 1), :].rearrange("p a d -> p (a d)"),
                                 xm[:, b % 2, :]).then_inc(s_xw[b % 2], 16)
                if real(i - ZERO_FROM, NE // ZERO):
                    if isinstance(i, int) and i == ZERO_FROM:
                        sp.wait_ge(s_zero, 2)
                        sp.wait_ge(s_k, N_K)
                    piece = i - ZERO_FROM
                    places = (xs[piece * ZERO * P:(piece + 1) * ZERO * P, :] if isinstance(i, int)
                              else xs[bass.ds(piece * (ZERO * P), ZERO * P), :])
                    sp.dma_start(places.rearrange("(t p) d -> p t d", p=P),
                                 pad_row[:].unsqueeze(1).broadcast_to([P, ZERO, W])).then_inc(s_zf, 16)

            over_attention(sp, attention_io)
            sp.wait_ge(s_lg, NT)
            for dst, src in ((tri, a["tri"]), (ones, a["ones"]), (j_idx, a["j_idx"]), (place_value, a["place_value"])):
                sp.dma_start(dst, src).then_inc(s_tri, 16)

            def load_rows(j, b):
                if real(j, NE):
                    ge(sp, ffn["ex"]["xt"], j - 3)
                    ge(sp, s_dest, j - 3)
                    sp.dma_start(rows_in[:, b, :], row_tile(xs, j)).then_inc(s_xs[b], 16)

            def expert_io(i, b):
                load_rows(i + 3, (b + 3) % 4)

            for done in s_sc1:
                sp.wait_ge(done, (NT - LATE) // NX * 32)
            sp.wait_ge(s_late, LATE * 32)
            for j in range(3):
                load_rows(j, j)
            over_tiles(sp, expert_io, NE, 4, ahead=3)

            def load_outputs(t, b):
                if real(t):
                    ge(sp, s_os[b], passes(t, b, 16, NG))
                    both_ranks = ys[0:2 * T, :].rearrange("(t r) d -> t (r d)", r=2)
                    sp.dma_start(g[:, b].rearrange("p r d -> p (r d)"), row_tile(both_ranks, t)).then_inc(s_g[b], 16)

            def store_out(t, b):
                if real(t):
                    sp.wait_ge(s_cmb, t + 1)
                    sp.dma_start(row_tile(out, t), g[:, b, 1, :]).then_inc(s_os[b], 16)

            AHEAD = NG - 2

            def combine_io(i, b):
                load_outputs(i + AHEAD, (b + AHEAD) % NG)
                store_out(i, b)

            for done in s_ys:
                sp.wait_ge(done, NE // 4 * 16)
            for t in range(AHEAD):
                load_outputs(t, t)
            over_tiles(sp, combine_io, unroll=NG, ahead=AHEAD)
            for done in s_os:
                sp.wait_ge(done, NT // NG * 16)

        @block.gpsimd
        def _(pool):
            pool.memset(ident[:], 0.0).then_inc(s_id, 1)
            pool.wait_ge(s_id, 1)
            pool.affine_select(out=ident[:], in_=ident[:], compare_op=ALU.not_equal, fill=1.0, base=0,
                               pattern=[[-1, P]], channel_multiplier=1).then_inc(s_id, 1)
            pool.memset(pad_row[:, 0:D], 0.0)
            pool.memset(c15[:], 1.5)
            pool.memset(vbd[:], 0.0).then_inc(s_zero, 1)
            pool.memset(yTs[0][:].bitcast(F32), 0.0).then_inc(s_yz, 1)
            pool.memset(yTs[1][:].bitcast(F32), 0.0).then_inc(s_yz, 1)
            pool.memset(rows_r[:].bitcast(F32), 0.0).then_inc(s_zero, 1)
            pool.wait_ge(s_yz, 2)

            def spread_y(t, b):
                ge(pool, s_yl[b], (t - b) * 8 + 16 if not isinstance(t, int) else (t // 2 + 1) * 16)
                ge(pool, s_proj, t - 1)
                settle(pool)
                yi = y_in[:, b, :].rearrange("p (s k) -> p s k", s=2)
                for n, (k0, k1) in enumerate(((0, NM), (NM, NK))):
                    m = pool.tensor_copy(yTs[0][:, b, n, :, k0:k1], yi[:, :, k0:k1])
                m.then_inc(s_yh, 1)
                pool.wait_ge(s_yh, t + 1)
                for n, (k0, k1) in enumerate(((0, NM), (NM, NK))):
                    m = pool.tensor_tensor(yTs[1][:, b, n, :, k0:k1], yi[:, :, k0:k1],
                                           yTs[0][:, b, n, :, k0:k1].bitcast(F32), ALU.subtract)
                m.then_inc(s_y, 1)

            def newton(t, b):
                pool.wait_ge(s_var, t + 1)
                y0 = seed[:, b, :].bitcast(F32)
                chain = t * 12
                for n in range(3):
                    src = y0 if n == 0 else ya[:, b, :]
                    if n:
                        pool.wait_ge(s_nw, chain + 4 * n)
                    pool.tensor_tensor(yt[:, b, :], src, src, ALU.mult).then_inc(s_nw, 1)
                    pool.wait_ge(s_nw, chain + 4 * n + 1)
                    pool.tensor_tensor(yt[:, b, :], yt[:, b, :], hv[:, b, :], ALU.mult).then_inc(s_nw, 1)
                    pool.wait_ge(s_nw, chain + 4 * n + 2)
                    pool.tensor_tensor(yt[:, b, :], yt[:, b, :], c15[:], ALU.add).then_inc(s_nw, 1)
                    pool.wait_ge(s_nw, chain + 4 * n + 3)
                    if n == 0:
                        ge(pool, s_qk, min(t - 1, NT) if isinstance(t, int) else t - 1)
                        ge(pool, s_n2, t - 6)
                    pool.tensor_tensor(ya[:, b, :], src, yt[:, b, :], ALU.mult).then_inc(s_nw, 1)
                pool.wait_ge(s_nw, chain + 12)
                pool.sem_inc(s_rs, 1)

            def normalise(t, b):
                pool.wait_ge(s_rd, t + 1)
                for n, (k0, k1) in enumerate(((0, NM), (NM, NK))):
                    p = S[:, b, :, :, k0:k1].rearrange("p g c k -> p (g c) k")
                    r = den[:, b, n, :].unsqueeze(2).broadcast_to([P, H, k1 - k0])
                    pool.tensor_tensor(p, p, r, ALU.mult).then_inc(s_nm, 1)

            def step(i, b):
                even, odd = b % 2, (b + 1) % 2
                if real(i + 3):
                    spread_y(i + 3, odd)
                if real(i + 2, NT + 5):
                    newton(i + 2, even)
                if real(i):
                    normalise(i, even)
                if real(i, NPIECE):
                    pool.wait_ge(s_high, i + 1)
                    settle(pool)
                    pool.tensor_tensor(at_tile(w_all[1], i, PIECE), stage[:, even, :],
                                       at_tile(w_all[0], i, PIECE).bitcast(F32), ALU.subtract).then_inc(s_split, 1)

            over_attention(pool, step)

            pool.wait_ge(s_zf, NE // ZERO * 16)
            pool.wait_ge(s_pos, 1)

            def scatter(row, places, sent):
                settle(pool)
                for n in range(2):
                    to = bass.IndirectOffsetOnAxis(ap=places[:, n:n + 1], axis=0)
                    pool.indirect_dma_start(xs, to, row, None).then_inc(sent, 16)

            def scatter_rows(i, b):
                if real(i, NT - LATE):
                    pool.wait_ge(ffn["sh"]["x"], i + 1)
                    scatter(x2_row[:, b, :], idx[:, b, :], s_sc1[b])
                if isinstance(i, int) and i in LATE_AFTER:
                    t = LATE_AFTER.index(i)
                    pool.wait_ge(ffn["late"]["x"], t + 1)
                    scatter(late_row[:, t, :], late_idx[:, t, :], s_late)

            over_tiles(pool, scatter_rows, NT - LATE, unroll=NX)

            def scatter_back(i, b):
                if real(i, NE):
                    pool.wait_ge(s_dest, i + 1)
                    pool.wait_ge(ffn["ex"]["yd"], i + 1)
                    settle(pool)
                    to = bass.IndirectOffsetOnAxis(ap=dest[:, b, 0:1], axis=0)
                    pool.indirect_dma_start(ys, to, y_sb[:, b, :], None).then_inc(s_ys[b], 16)

            over_tiles(pool, scatter_back, NE, 4)

        @block.scalar
        def _(act):
            act.wait_ge(s_w, N_W)
            act.activation(masks_r[:], row_masks, ACT.Copy)
            act.wait_ge(s_cen, 1)
            act.wait_ge(s_zero, 2)
            act.activation(rows_r[0:4, :], rows, ACT.Copy).then_inc(s_rh, 1)
            for n in range(2):
                act.activation(proj[0][:, 4 * n:4 * n + 4], w_in[:, 4 * n:4 * n + 4], ACT.Copy).then_inc(s_wh, 1)
            act.wait_ge(s_st, 1)
            act.activation(rstd1[:, 0:Q], rstd1[:, 0:Q], ACT.Sqrt).then_inc(s_rt, 1)

            def step(i, b):
                even, odd = b % 2, (b + 1) % 2
                if real(i + 2):
                    t = i + 2
                    act.wait_ge(s_pqk, t + 1)
                    ge(act, s_vr, t)
                    act.activation(sq, pQK[:], ACT.Square).then_inc(s_sq, 1)
                    ge(act, s_tq, t - 1)
                    act.activation(qk[:, even, :], pQK[:], ACT.Copy).then_inc(s_raw, 1)
                if real(i):
                    act.wait_ge(s_mx, 2 * (i + 1))
                    act.activation(S[:, even], S[:, even], ACT.Exp, scale=SCALE).then_inc(s_ex, 1)
                if real(i - 1):
                    t = i - 1
                    act.wait_ge(s_pt, t + 1)
                    ge(act, s_pv, t)
                    act.activation(PT.rearrange("p g c n -> p g (c n)"), p_pt, ACT.Copy).then_inc(s_pe, 1)
                if real(i + 1):
                    t = i + 1
                    act.wait_ge(s_tq, t + 1)
                    ge(act, s_sc, t - 1)
                    act.activation(qT[:, odd].rearrange("p c n -> p (c n)"), pT[:, 0].rearrange("p c n -> p (c n)"),
                                   ACT.Identity, scale=vecs[:, 0:1], bias=vecs[:, 1:2])
                    for par in range(2):
                        for n, (k0, k1) in enumerate(((0, NM), (NM, NK))):
                            m = act.activation(
                                kT[:, odd, :, par, :, k0:k1],
                                pT[:, 1].rearrange("p c (s k) -> p c s k", s=2)[:, :, :, k0:k1],
                                ACT.Identity, scale=kvec[:, par, 2 * n:2 * n + 1], bias=kvec[:, par, 2 * n + 1:2 * n + 2])
                    m.then_inc(s_qe, 1)
                if real(i, NPIECE):
                    n = (i - even) * 8 + 16 if not isinstance(i, int) else (i // 2 + 1) * 16
                    act.wait_ge(s_ws[even], n)
                    settle(act)
                    act.activation(at_tile(w_all[0], i, PIECE), stage[:, even, :], ACT.Copy).then_inc(s_high, 1)
                if real(i - 1):
                    t = i - 1
                    act.wait_ge(s_pv, t + 1)
                    ge(act, s_wo, t - 1)
                    act.activation(hTs[0][:, odd, 0:DC], p_c, ACT.Copy).then_inc(s_ch, 1)
                if real(i - 4):
                    act.wait_ge(s_t2, i - 3)
                    if real(i + 3):
                        act.wait_ge(s_tx, i + 4)
                    ge(act, s_lg, i - 4)
                    act.activation(x2aT.rearrange("p c n -> p (c n)"), pT[:, 1].rearrange("p c n -> p (c n)"),
                                   ACT.Copy).then_inc(s_e2, 1)
                if real(i + 3):
                    t = i + 3
                    act.wait_ge(s_tx, t + 1)
                    ge(act, s_pqk, t - 1)
                    act.activation(xTs[0][:, odd].rearrange("p c n -> p (c n)"), p_x, ACT.Copy).then_inc(s_xh, 1)
                if real(i + 2):
                    t = i + 2
                    act.wait_ge(s_proj, t + 1)
                    ge(act, s_pv, t - 3)
                    pairs = p_v.rearrange("p (j h d) -> p j h d", h=2, d=HD)
                    for s in range(2):
                        for par in range(2):
                            m = act.activation(vbd[64 * par:64 * par + 64, (b + 2) % 4, s, :, par, :],
                                               pairs[64 * s:64 * s + 64, :, par, :], ACT.Copy)
                    m.then_inc(s_vev, 1)

            def attention(i, b):
                step(i, b)
                if isinstance(i, int) and i == -1:
                    act.wait_ge(s_st, 2)
                    act.activation(rstd1[:, Q:NT], rstd1[:, Q:NT], ACT.Sqrt).then_inc(s_rt, 1)
                    act.activation(tg[:], gates[:], ACT.Tanh).then_inc(s_tg, 1)

            over_attention(act, attention)

            act.wait_ge(s_rx, 1)
            act.activation(lg, lg, ACT.Exp).then_inc(s_re, 1)
            ffn_act(act, "sh", NT - LATE)
            ffn_act(act, "ex", NE)
            ffn_act(act, "late", LATE)

        @block.tensor
        def _(pe):
            def parts(dst, pairs, bias=None):
                for m, ((xh, xl), (wh, wl)) in enumerate(pairs):
                    pe.matmul(dst, xh, wl, start=(m == 0), stop=False)
                    pe.matmul(dst, xl, wh, start=False, stop=False)
                    pe.matmul(dst, xh, wh, start=False, stop=False)
                return pe.matmul(dst, masks_r[:], rows_r[:, bias * D:(bias + 1) * D], start=False, stop=True)

            def project(t, b):
                pe.wait_ge(s_xl, t + 1)
                pe.wait_ge(s_y, t + 1)
                ge(pe, s_raw, t)
                w = lambda n: [p[:, n, :] for p in proj]
                x = [[p[:, b, c, :] for p in xTs] for c in range(DC)]
                y = [[p[:, b, n].rearrange("p s k -> p (s k)") for p in yTs] for n in range(2)]
                parts(pQK[:, 0:D], [(x[c], w(WQ + c)) for c in range(DC)], 0)
                parts(pQK[:, D:2 * D], [(y[0], w(WKM)), (y[1], w(WKD))], 1).then_inc(s_pqk, 1)

            def project_v(t, b):
                ge(pe, s_vev, t)
                y = [[p[:, b, n].rearrange("p s k -> p (s k)") for p in yTs] for n in range(2)]
                parts(p_v, [(y[n], [p[:, w, :] for p in proj]) for n, w in enumerate((WVM, WVD))], 2).then_inc(s_proj, 1)

            def step(i, b):
                even, odd = b % 2, (b + 1) % 2
                if real(i):
                    pe.wait_ge(s_qe, i + 1)
                    ge(pe, s_mx, 2 * i)
                    ge(pe, s_pe, i - 1)
                    for c in range(DC):
                        for s in range(2):
                            for g in range(G):
                                m = pe.matmul(p_sc[64 * s:64 * s + 64, g, c * P:(c + 1) * P],
                                              qT[32 * g:32 * g + 32, even, c, 64 * s:64 * s + 64],
                                              kT[32 * g:32 * g + 32, even, c, :, s, :], start=True, stop=True)
                    m.then_inc(s_sc, 1)
                if real(i + 2):
                    project(i + 2, even)
                if real(i - 2):
                    t = i - 2
                    pe.wait_ge(s_cl, t + 1)
                    parts(p_o, [([h[:, even, c] for h in hTs], [p[:, WO + c, :] for p in proj]) for c in range(DC)],
                          3).then_inc(s_wo, 1)
                if real(i - 1):
                    t = i - 1
                    pe.wait_ge(s_nm, 2 * (t + 1))
                    if real(i):
                        pe.wait_ge(s_mx, 2 * (i + 1))
                    for g in range(G):
                        for c in range(DC):
                            m = pe.transpose(p_pt[:, g, c * P:(c + 1) * P],
                                             S[:, odd, g, 2 * c:2 * c + 2, :].rearrange("p h k -> p (h k)"), ident[:])
                    m.then_inc(s_pt, 1)
                if real(i + 1):
                    t = i + 1
                    pe.wait_ge(s_qk, t + 1)
                    if real(i + 2):
                        pe.wait_ge(s_xl, i + 3)
                    if real(i - 5):
                        pe.wait_ge(s_e2, i - 4)
                    for n in range(2):
                        for c in range(DC):
                            m = pe.transpose(pT[:, n, c, :], qk[:, odd, n * D + c * P:n * D + (c + 1) * P], ident[:])
                    m.then_inc(s_tq, 1)
                if real(i - 1):
                    t = i - 1
                    pe.wait_ge(s_pe, t + 1)
                    ge(pe, s_res, t)
                    for s in range(2):
                        for c in range(DC):
                            for g in range(G):
                                m = pe.matmul(p_c[32 * g:32 * g + 32, c, 64 * s:64 * s + 64],
                                              vbd[:, (b - 1) % 4, s, G * c + g].rearrange("p h d -> p (h d)"),
                                              PT[:, g, c, 64 * s:64 * s + 64], start=True, stop=True)
                    m.then_inc(s_pv, 1)
                if real(i - 5):
                    pe.wait_ge(s_e2, i - 4)
                    ge(pe, s_vev, min(i + 2, NT) if isinstance(i, int) else i + 2)
                    if isinstance(i, int) and i == 5:
                        pe.wait_ge(s_k, N_K)
                    for c in range(DC):
                        m = pe.matmul(at_tile(p_logits, i - 5, E), x2aT[:, c, :], gateT[:, c, :],
                                      start=(c == 0), stop=(c == DC - 1))
                    m.then_inc(s_lg, 1)
                if real(i + 2):
                    project_v(i + 2, even)
                if real(i - 4):
                    pe.wait_ge(s_n2, i - 3)
                    ge(pe, s_qe, min(i + 2, NT) if isinstance(i, int) else i + 2)
                    ge(pe, s_e2, i - 4)
                    for c in range(DC):
                        m = pe.transpose(pT[:, 1, c, :], x2a[:, c * P:(c + 1) * P], ident[:])
                    m.then_inc(s_t2, 1)
                if real(i + 3):
                    t = i + 3
                    pe.wait_ge(s_xn, t + 1)
                    ge(pe, s_qe, t - 1)
                    for c in range(DC):
                        m = pe.transpose(p_x[:, c * P:(c + 1) * P], xn[:, odd, c * P:(c + 1) * P], ident[:])
                    m.then_inc(s_tx, 1)

            pe.wait_ge(s_id, 2)
            pe.wait_ge(s_tidy, 3)
            over_attention(pe, step)

            def counts():
                pe.wait_ge(s_oh, 1)
                pe.wait_ge(s_tri, 4 * 16)
                flat = both.rearrange("p t e -> p (t e)")
                pe.matmul(bank[7][:, 0:NT * E], tri, flat, start=True, stop=True)
                pe.matmul(bank[7][:, NT * E:2 * NT * E], ones, flat, start=True, stop=True).then_inc(s_cnt, 1)

            pe.wait_ge(s_split, NPIECE)
            ffn_pe(pe, "sh", NT - LATE, after={1: [counts]})
            ffn_pe(pe, "ex", NE)
            ffn_pe(pe, "late", LATE)

        @block.vector
        def _(dve):
            dve.wait_ge(s_w, N_W)
            cases = [(w_in[:, n, :], csum[:, m, :]) for m, n in enumerate((WQ, WQ + 1, WKM, WKD))]
            cases.append((rows[:, 0:2 * D], bsum[:]))
            for w, s in cases:
                dve.tensor_reduce(s, heads(w), AX.X, ALU.add).then_inc(s_c, 1)
            dve.wait_ge(s_c, 5)
            dve.tensor_scalar(csum[:, 0:4], csum[:, 0:4], 1.0 / HD, None, ALU.mult).then_inc(s_c, 1)
            dve.tensor_scalar(bsum[:], bsum[:], 1.0 / HD, None, ALU.mult).then_inc(s_c, 1)
            dve.wait_ge(s_c, 7)
            for w, s in cases:
                n = s.shape[1]
                dve.tensor_tensor(heads(w), heads(w), s.unsqueeze(2).broadcast_to([w.shape[0], n, HD]), ALU.subtract)
            for par in range(2):
                m = dve.tensor_scalar(kvec[:, par, :], vecs[:, 2:6], par_mask[:, par:par + 1], None, ALU.mult)
            m.then_inc(s_cen, 1)

            def ln1_stats(n):
                dve.wait_ge(s_x[n], 16)
                for t in range(n * Q, (n + 1) * Q):
                    m = dve.bn_stats(st1[:, t, :], X[:, t, :])
                m.then_inc(s_bn, 1)
                dve.wait_ge(s_bn, n + 1)
                for t in range(n * Q, (n + 1) * Q):
                    m = dve.bn_aggr(mv1[:, t, :], st1[:, t, :])
                m.then_inc(s_mv, 1)

            def ln1_var(k0, k1):
                dve.tensor_scalar(rstd1[:, k0:k1], mv1[:, k0:k1, 1], 1e-5, None, ALU.add).then_inc(s_st, 1)

            ln1_stats(0)
            dve.wait_ge(s_mv, 1)
            ln1_var(0, Q)
            dve.wait_ge(s_cen, 1)
            dve.wait_ge(s_rh, 1)
            dve.tensor_tensor(rows_r[32:36, :], rows, rows_r[0:4, :].bitcast(F32), ALU.subtract).then_inc(s_tidy, 1)
            for n in range(2):
                dve.wait_ge(s_wh, n + 1)
                dve.tensor_tensor(proj[1][:, 4 * n:4 * n + 4], w_in[:, 4 * n:4 * n + 4],
                                  proj[0][:, 4 * n:4 * n + 4].bitcast(F32), ALU.subtract).then_inc(s_tidy, 1)
            dve.wait_ge(s_rt, 1)
            dve.reciprocal(rstd1[:, 0:Q], rstd1[:, 0:Q]).then_inc(s_r1, 1)
            dve.wait_ge(s_r1, 1)

            def norm_x(t, b):
                ge(dve, s_tx, t - 1)
                dve.tensor_scalar(xn[:, b, :], X[:, t, :], mv1[:, t, 0:1], at_tile(rstd1, t),
                                  ALU.subtract, ALU.mult).then_inc(s_xn, 1)

            def variances(t, b):
                if real(t):
                    dve.wait_ge(s_sq, t + 1)
                ge(dve, s_rs, t - 1)
                if real(t - 5):
                    dve.wait_ge(s_mvr, t - 4)
                    dve.tensor_scalar(var[:, b, 2 * H:], mvr[:, (b + 1) % 2, 1:2], float(HD), 9e-6 * HD,
                                      ALU.mult, ALU.add).then_inc(s_v2, 1)
                if real(t):
                    dve.tensor_reduce(var[:, b, 0:2 * H], heads(sq), AX.X, ALU.add).then_inc(s_vr, 1)
                    dve.wait_ge(s_vr, t + 1)
                if real(t - 5):
                    dve.wait_ge(s_v2, t - 4)
                dve.tensor_scalar(hv[:, b, :], var[:, b, :], -0.5 / HD, -0.5e-6, ALU.mult, ALU.add).then_inc(s_seed, 1)
                dve.tensor_scalar(seed[:, b, :].bitcast(F32), var[:, b, :], 1.0 / HD, 1e-6,
                                  ALU.mult, ALU.add).then_inc(s_seed, 1)
                dve.wait_ge(s_seed, 2 * t + 2)
                dve.tensor_scalar(seed[:, b, :], seed[:, b, :], -0.5, float(RSQRT_SEED), ALU.mult, ALU.add).then_inc(s_var, 1)

            def step(i, b):
                even, odd = b % 2, (b + 1) % 2
                if real(i):
                    dve.wait_ge(s_sc, i + 1)
                    ge(dve, s_pt, i - 1)
                    sc = p_sc.rearrange("p g (c k) -> p g c k", k=NK)
                    for n, (k0, k1) in enumerate(((0, NM), (NM, NK))):
                        dve.tensor_reduce(mx[:, even, n], sc[:, :, :, k0:k1], AX.X, ALU.max).then_inc(s_max, 1)
                    for n, (k0, k1) in enumerate(((0, NM), (NM, NK))):
                        dve.wait_ge(s_max, 2 * i + 1 + n)
                        dve.tensor_tensor(S[:, even, :, :, k0:k1], sc[:, :, :, k0:k1],
                                          mx[:, even, n].unsqueeze(3).broadcast_to([P, G, 4, k1 - k0]),
                                          ALU.subtract).then_inc(s_mx, 1)
                if real(i + 1):
                    t = i + 1
                    dve.wait_ge(s_rs, t + 1)
                    dve.wait_ge(s_raw, t + 1)
                    dve.tensor_tensor(heads(qk[:, odd, :]), heads(qk[:, odd, :]),
                                      ya[:, odd, 0:2 * H].unsqueeze(2).broadcast_to([P, 2 * H, HD]), ALU.mult).then_inc(s_qk, 1)
                if real(i - 2):
                    t = i - 2
                    dve.wait_ge(s_wo, t + 1)
                    ge(dve, s_xw[b % 2], passes(t, b % 2, 16, 2))
                    dve.scalar_tensor_tensor(out=xm[:, even, :], in0=p_o, scalar=tg[:, 0:1], in1=X[:, t, :],
                                             op0=ALU.mult, op1=ALU.add).then_inc(s_res, 1)
                if real(i + 2, NT + 5):
                    variances(i + 2, even)
                if real(i - 4):
                    t = i - 4
                    dve.wait_ge(s_rs, i + 2)
                    dve.wait_ge(s_l2, t + 1)
                    dve.wait_ge(s_xw[b % 2], passes(t, b % 2, 16, 2) + 16)
                    ge(dve, s_t2, t)
                    dve.tensor_scalar(rstd2[:, t:t + 1] if isinstance(t, int) else rstd2[:, bass.ds(t, 1)],
                                      ya[:, odd, 2 * H:], 1.0, None, ALU.mult)
                    dve.tensor_scalar(x2a, X[:, t, :], mv2[:, t, 0:1], ya[:, odd, 2 * H:],
                                      ALU.subtract, ALU.mult).then_inc(s_n2, 1)
                if real(i):
                    dve.wait_ge(s_ex, i + 1)
                    ge(dve, s_nm, 2 * (i - 1))
                    for n, (k0, k1) in enumerate(((0, NM), (NM, NK))):
                        dve.tensor_reduce(den[:, even, n, :], S[:, even, :, :, k0:k1].rearrange("p g c k -> p (g c) k"),
                                          AX.X, ALU.add).then_inc(s_sum, 1)
                    dve.wait_ge(s_sum, 2 * (i + 1))
                    dve.reciprocal(den[:, even], den[:, even]).then_inc(s_rd, 1)
                if real(i + 4):
                    norm_x(i + 4, even)
                if real(i - 2):
                    t = i - 2
                    dve.wait_ge(s_res, t + 1)
                    dve.bn_stats(st2[:, even, :], xm[:, even, :]).then_inc(s_b2, 1)
                if real(i - 1) or real(i - 2):
                    if real(i - 2):
                        dve.wait_ge(s_b2, i - 1)
                    if real(i - 1):
                        dve.wait_ge(s_ch, i)
                        dve.tensor_tensor(hTs[1][:, odd, 0:DC], p_c, hTs[0][:, odd, 0:DC].bitcast(F32),
                                          ALU.subtract).then_inc(s_cl, 1)
                    if real(i - 2):
                        dve.bn_aggr(mvr[:, even, :], st2[:, even, :]).then_inc(s_mvr, 1)
                if real(i + 3):
                    dve.wait_ge(s_xh, i + 4)
                    dve.tensor_tensor(xTs[1][:, odd].rearrange("p c n -> p (c n)"), p_x,
                                      xTs[0][:, odd].rearrange("p c n -> p (c n)").bitcast(F32), ALU.subtract).then_inc(s_xl, 1)
                if real(i - 3):
                    dve.wait_ge(s_mvr, i - 2)
                    dve.tensor_scalar(mv2[:, i - 3, :], mvr[:, odd, :], 1.0, None, ALU.mult).then_inc(s_l2, 1)

            dve.memset(var, 1.0).then_inc(s_v1, 1)
            dve.wait_ge(s_v1, 1)
            norm_x(0, 0)

            def attention(i, b):
                step(i, b)
                if isinstance(i, int) and i < 0:
                    ln1_stats(i + 4)
                if isinstance(i, int) and i == -1:
                    dve.wait_ge(s_mv, 4)
                    ln1_var(Q, NT)
                if isinstance(i, int) and i == 0:
                    dve.wait_ge(s_rt, 2)
                    dve.reciprocal(rstd1[:, Q:NT], rstd1[:, Q:NT]).then_inc(s_r1, 1)
                    dve.wait_ge(s_r1, 2)
                    dve.wait_ge(s_tg, 1)

            over_attention(dve, attention)

            dve.wait_ge(s_k, N_K)

            def norm_2(i, dst):
                return dve.tensor_scalar(dst, X[:, i, :], mv2[:, i, 0:1],
                                         rstd2[:, i:i + 1] if isinstance(i, int) else rstd2[:, bass.ds(i, 1)],
                                         ALU.subtract, ALU.mult)

            def x2_again(i, b):
                ge(dve, ffn["sh"]["xt"], i - NX + 1)
                ge(dve, s_sc1[b], passes(i, b, 32, NX))
                m = norm_2(i, x2_row[:, b, 0:D])
                if not isinstance(i, int) or i >= EARLY:
                    m = dve.tensor_scalar(x2_row[:, b, D:W], token_e1[:, i, :], 1.0, None, ALU.mult)
                if not isinstance(i, int) or i >= UNPLACED:
                    m = dve.tensor_copy(idx[:, b, :], pos[:, i, :])
                m.then_inc(ffn["sh"]["x"], 1)

            def late_rows(t0, t1):
                t = NT - LATE
                dve.tensor_scalar(late_row[:, t0:t1, D:W], token_e1[:, t + t0:t + t1, :], 1.0, None, ALU.mult)
                dve.tensor_copy(late_idx[:, t0:t1, :], pos[:, t + t0:t + t1, :])
                for n in range(t0, t1):
                    norm_2(t + n, late_row[:, n, 0:D]).then_inc(ffn["late"]["x"], 1)

            exponents, choose, prefix, starts, positions, weights, tile_experts = router(dve)
            exponents()
            ffn_dve(dve, "sh", NT - LATE, x2_again,
                    after={0: [choose], 1: [prefix], 2: [starts], 3: [positions], 4: [lambda: late_rows(0, LATE // 2)],
                           5: [weights], 6: [lambda: late_rows(LATE // 2, LATE)], 7: [tile_experts]})
            ffn_dve(dve, "ex", NE, None)
            dve.tensor_scalar(w1, w1, tg[:, 1:2], None, ALU.mult).then_inc(s_o1, 1)
            dve.tensor_scalar(w2, w2, tg[:, 1:2], None, ALU.mult).then_inc(s_o1, 1)
            dve.wait_ge(s_o1, 2)

            def combine(i, b):
                if real(i):
                    dve.wait_ge(s_g[b], passes(i, b, 16, NG) + 16)
                    dve.scalar_tensor_tensor(out=g[:, b, 0, :], in0=g[:, b, 0, :], scalar=at_tile(w1, i), in1=X[:, i, :],
                                             op0=ALU.mult, op1=ALU.add).then_inc(s_o1, 1)
                    dve.wait_ge(s_o1, i + 3)
                    dve.scalar_tensor_tensor(out=g[:, b, 1, :], in0=g[:, b, 1, :], scalar=at_tile(w2, i),
                                             in1=g[:, b, 0, :], op0=ALU.mult, op1=ALU.add).then_inc(s_cmb, 1)

            each = (NT - LATE) // LATE
            ffn_dve(dve, "late", LATE, None,
                    after={n: [lambda t=t: combine(t, t % NG) for t in range(n * each, (n + 1) * each)]
                           for n in range(LATE)})
            for t in range(NT - LATE, NT):
                combine(t, t % NG)


def layout(np, i):
    f = lambda n: np.asarray(i[n])
    T, D = 4096, 256
    HD = 16
    wkv = np.concatenate([f("L0_xattn_Wk"), f("L0_xattn_Wv")], axis=1).reshape(128, 16, 2, HD)
    bkv = np.concatenate([f("L0_xattn_bk"), f("L0_xattn_bv")]).reshape(16, 2, HD)
    wd = f("L0_xattn_Wkv_dca").reshape(128, 2, 16, HD)
    bd = f("L0_xattn_bkv_dca").reshape(2, 16, HD)
    flat = lambda w: np.ascontiguousarray(w.reshape(w.shape[0], -1))
    rows = np.zeros((4, 4, D), np.float32)
    rows[0, 0] = f("L0_xattn_bq")
    rows[1, 1], rows[2, 1] = bkv[:, 0].ravel(), bd[0].ravel()
    rows[1, 2], rows[2, 2] = bkv[:, 1].ravel(), bd[1].ravel()
    rows[0, 3] = f("L0_xattn_bo")
    masks = np.zeros((64, 2, 64), np.float32)
    for r in (0, 32):
        masks[r] = 1
        masks[r + 1, :, :48] = 1
        masks[r + 2, :, 48:] = 1
    vec = [np.tile(f("L0_xattn_" + n), 8) for n in ("qn_w", "qn_b", "kn_w", "kn_b", "kn_dca_w", "kn_dca_b")]
    par = (np.arange(128) // HD % 2)
    def lay(w):
        k = w.shape[0]
        w = np.concatenate([w, np.zeros((-k % 128,) + w.shape[1:], w.dtype)])
        return np.ascontiguousarray(w.reshape(-1, 128, *w.shape[1:]).swapaxes(0, 1)).reshape(128, -1)
    w_all = np.concatenate([
        lay(np.concatenate([f("L0_ffn_w_gate"), f("L0_ffn_w_up")], axis=1).transpose(2, 0, 1)),
        lay(f("L0_ffn_w_down").transpose(2, 0, 1)),
        lay(np.concatenate([f("L0_ffn_sw_gate"), f("L0_ffn_sw_up")], axis=0).T),
        lay(f("L0_ffn_sw_down").T)], axis=1)
    return {
        "x": f("x").reshape(T, D), "ctxT": np.ascontiguousarray(f("ctx_1024").reshape(T, 128).T),
        "wq": f("L0_xattn_Wq"), "wkv": np.stack([flat(w) for w in (wkv[:, :, 0], wkv[:, :, 1], wd[:, 0], wd[:, 1])]),
        "wo": f("L0_xattn_Wo"),
        "rows": rows.reshape(4, 4 * D), "row_masks": masks.reshape(64, 128),
        "vecs": np.stack(vec, axis=1), "par_mask": np.stack([1 - par, par], 1).astype(np.float32),
        "g_xattn": f("g_xattn"), "g_ffn": f("g_ffn"),
        "gateT": np.ascontiguousarray(f("L0_ffn_gate_weight").T),
        "w_all": w_all,
        "tri": np.triu(np.ones((128, 128), np.float32), 1), "ones": np.ones((128, 128), np.float32),
        "e_idx": np.tile(np.arange(8, dtype=np.float32), (128, 1)),
        "place_value": np.tile(8.0 ** (np.arange(72) % 8), (128, 1)).astype(np.float32),
        "tok_idx": 2 * np.arange(T, dtype=np.float32).reshape(32, 128).T,
        "pad": np.stack([2 * T - 1 + np.arange(128), np.full(128, -1)], axis=1).astype(np.float32),
        "j_idx": np.tile(np.arange(72, dtype=np.float32), (128, 1)),
    }


def kernel(**inputs):
    import numpy as _np
    import concourse.bacc as _bacc
    from concourse.bass_utils import run_bass_kernel_spmd as _run

    nc = _bacc.Bacc("TRN2", target_bir_lowering=False, num_devices=1)
    arrays, aps = {}, {}
    for name, array in layout(_np, inputs).items():
        array = _np.ascontiguousarray(array)
        arrays[f"in_{name}_dram"] = array
        aps[name] = nc.dram_tensor(f"in_{name}_dram", array.shape, mybir.dt.from_np(array.dtype),
                                   kind="ExternalInput").ap()
    out = nc.dram_tensor("out_dram", (4096, 256), F32, kind="ExternalOutput").ap()
    gated_cross_attention_and_moe(nc, aps, out)
    r = _run(nc, [arrays], core_ids=[0])
    return r.results[0]["out_dram"].reshape(64, 64, 256)
```
